# Optimizing a Trainium2 kernel written in Bass

```python
import numpy as np
import jax
import jax.numpy as jnp

def _softmax(x, axis=-1):
    return jax.nn.softmax(x, axis=axis)

def _gelu(x):
    return jax.nn.gelu(x, approximate=True)

def _silu(x):
    return jax.nn.silu(x)

def _sigmoid(x):
    return jax.nn.sigmoid(x)

def _layernorm(x, axis=-1, eps=1e-05):
    m = jnp.mean(x, axis=axis, keepdims=True)
    v = jnp.var(x, axis=axis, keepdims=True)
    return (x - m) / jnp.sqrt(v + eps)

def _scatter_add(tgt, idx, src, axis=0):
    return tgt.at[idx].add(src)

def _segment_sum(src, seg, n):
    return jax.ops.segment_sum(src, seg, n)
kernel_name = 'mk_flamingo_gated_d1_seqx_r8_79acd5'

def setup_inputs(seed: int=0):
    np.random.seed(seed)
    _w = jnp.asarray

    def _rec_inputs():
        import jax
        import jax.numpy as jnp
        _rk = jax.random.key(seed)
        x = -0.0002928 + 1 * jax.random.normal(jax.random.fold_in(_rk, 1), (2, 512, 128), jnp.float32)
        _lenS = 512 - jax.random.randint(jax.random.fold_in(_rk, 7), (2,), 0, max(1, 512 // 4) + 1, jnp.int32)
        _lenS2 = 154 - jax.random.randint(jax.random.fold_in(_rk, 8), (2,), 0, max(1, 154 // 4) + 1, jnp.int32)
        _ctx_1024P = jax.random.normal(jax.random.fold_in(_rk, 11), (2, 16, 128), jnp.float32)
        _ctx_1024c = jax.random.dirichlet(jax.random.fold_in(_rk, 511), 0.3 * jnp.ones((16,), jnp.float32), (2, 154))
        _ctx_1024t = jnp.einsum('bsk,bkd->bsd', _ctx_1024c, _ctx_1024P)
        _ctx_1024t = _ctx_1024t * jax.lax.rsqrt(jnp.mean(jnp.square(_ctx_1024t)) + 1e-12) * 0.953939
        ctx_1024 = -1.39393e-06 + 0.999914 * (_ctx_1024t + 0.3 * jax.random.normal(jax.random.fold_in(_rk, 611), (2, 154, 128), jnp.float32))
        _g = jax.random.normal(jax.random.fold_in(_rk, 9001), (2, 1), jnp.float32)
        _g = jnp.sign(_g) * jnp.maximum(jnp.abs(_g), 1.0) + (_g == 0) * 1.0
        g_xattn = _g[0]
        g_ffn = _g[1]
        return (x, ctx_1024, g_xattn, g_ffn)
    x, ctx_1024, g_xattn, g_ffn = _rec_inputs()

    def _L0_xattn_setup():
        import jax, jax.numpy as jnp
        import numpy as np
        EMBED_DIM = 128
        NUM_HEADS = 16
        HEAD_DIM = EMBED_DIM // NUM_HEADS
        key = jax.random.key(seed)
        ks = jax.random.split(key, 7)
        B, S, E = (2, 256, EMBED_DIM)
        scale = 1.0 / np.sqrt(E)
        return {'query': jax.random.normal(ks[0], (B, S, E), dtype=jnp.float32), 'key': jax.random.normal(ks[1], (B, S, E), dtype=jnp.float32), 'value': jax.random.normal(ks[2], (B, S, E), dtype=jnp.float32), 'Wq': jax.random.normal(ks[3], (E, E), dtype=jnp.float32) * scale, 'Wk': jax.random.normal(ks[4], (E, E), dtype=jnp.float32) * scale, 'Wv': jax.random.normal(ks[5], (E, E), dtype=jnp.float32) * scale, 'Wo': jax.random.normal(ks[6], (E, E), dtype=jnp.float32) * scale}
    _L0_xattn_all = _L0_xattn_setup()
    _L0_xattn_in = {k: v for k, v in _L0_xattn_all.items() if k in ('Wq', 'Wk', 'Wv', 'Wo')}
    del _L0_xattn_all

    def _L0_ffn_setup():
        import jax, jax.numpy as jnp
        import numpy as np
        DIM = 128
        N_EXPERTS = 8
        TOPK = 2
        CAPACITY_FACTOR = 1.25
        B, S = (2, 256)

        def _moe(x, Wr, W1, b1, W2, b2):
            Bsz, Sl, D = x.shape
            E = Wr.shape[1]
            T = Bsz * Sl
            capacity = max(1, int(T * CAPACITY_FACTOR / E))
            xt = x.reshape(T, D)
            probs_full = jax.nn.softmax(xt @ Wr, axis=-1)
            topv, topi = jax.lax.top_k(probs_full, TOPK)
            topv = topv / jnp.sum(topv, axis=-1, keepdims=True)
            onehot = jax.nn.one_hot(topi, E, dtype=x.dtype)
            rank = jnp.cumsum(onehot, axis=0)
            keep = (rank <= capacity).astype(x.dtype) * onehot
            w = jnp.einsum('tk,tke->te', topv, keep)
            h = jax.nn.gelu(jnp.einsum('td,edf->etf', xt, W1) + b1[:, None, :], approximate=False)
            y = jnp.einsum('etf,efd->etd', h, W2) + b2[:, None, :]
            out = jnp.einsum('te,etd->td', w, y)
            return out.reshape(Bsz, Sl, D)
        key = jax.random.key(seed)
        ks = jax.random.split(key, 6)
        D, E, F = (DIM, N_EXPERTS, 4 * DIM)
        x = jax.random.normal(ks[0], (B, S, D), dtype=jnp.float32)
        Wr = jax.random.normal(ks[1], (D, E), dtype=jnp.float32) * (1.0 / np.sqrt(D))
        W1 = jax.random.normal(ks[2], (E, D, F), dtype=jnp.float32) * (1.0 / np.sqrt(D))
        b1 = jnp.zeros((E, F), dtype=jnp.float32)
        W2 = jax.random.normal(ks[3], (E, F, D), dtype=jnp.float32) * (1.0 / np.sqrt(F))
        b2 = jnp.zeros((E, D), dtype=jnp.float32)
        return {'x': x, 'Wr': Wr, 'W1': W1, 'b1': b1, 'W2': W2, 'b2': b2}
    _L0_ffn_all = _L0_ffn_setup()
    _L0_ffn_in = {k: v for k, v in _L0_ffn_all.items() if k in ('Wr', 'W1', 'b1', 'W2', 'b2')}
    del _L0_ffn_all
    return {'x': x, 'ctx_1024': ctx_1024, 'g_xattn': g_xattn, 'g_ffn': g_ffn, 'L0_xattn_Wq': _L0_xattn_in['Wq'], 'L0_xattn_Wk': _L0_xattn_in['Wk'], 'L0_xattn_Wv': _L0_xattn_in['Wv'], 'L0_xattn_Wo': _L0_xattn_in['Wo'], 'L0_ffn_Wr': _L0_ffn_in['Wr'], 'L0_ffn_W1': _L0_ffn_in['W1'], 'L0_ffn_b1': _L0_ffn_in['b1'], 'L0_ffn_W2': _L0_ffn_in['W2'], 'L0_ffn_b2': _L0_ffn_in['b2']}

def reference(x, ctx_1024, g_xattn, g_ffn, L0_xattn_Wq, L0_xattn_Wk, L0_xattn_Wv, L0_xattn_Wo, L0_ffn_Wr, L0_ffn_W1, L0_ffn_b1, L0_ffn_W2, L0_ffn_b2):
    import jax
    import jax.numpy as jnp

    def _L0_xattn_ref(query, key, value, Wq, Wk, Wv, Wo):
        import jax, jax.numpy as jnp
        import numpy as np
        EMBED_DIM = 128
        NUM_HEADS = 16
        HEAD_DIM = EMBED_DIM // NUM_HEADS
        B, Sq, E = query.shape
        Sk = key.shape[1]
        H, D = (NUM_HEADS, HEAD_DIM)

        def split_heads(x, S):
            return x.reshape(B, S, H, D).transpose(0, 2, 1, 3)
        Q = split_heads(query @ Wq.T, Sq)
        K = split_heads(key @ Wk.T, Sk)
        V = split_heads(value @ Wv.T, Sk)
        scores = jnp.einsum('bhqd,bhkd->bhqk', Q, K) / jnp.sqrt(jnp.float32(D))
        causal = jnp.tril(jnp.ones((Sq, Sk), dtype=bool))
        scores = jnp.where(causal[None, None, :, :], scores, -jnp.inf)
        attn = jax.nn.softmax(scores, axis=-1)
        attn = jnp.nan_to_num(attn, nan=0.0)
        out = jnp.einsum('bhqk,bhkd->bhqd', attn, V)
        out = out.transpose(0, 2, 1, 3).reshape(B, Sq, E)
        return out @ Wo.T

    def _L0_ffn_ref(x, Wr, W1, b1, W2, b2):
        import jax, jax.numpy as jnp
        import numpy as np
        DIM = 128
        N_EXPERTS = 8
        TOPK = 2
        CAPACITY_FACTOR = 1.25
        B, S = (2, 256)

        def _moe(x, Wr, W1, b1, W2, b2):
            Bsz, Sl, D = x.shape
            E = Wr.shape[1]
            T = Bsz * Sl
            capacity = max(1, int(T * CAPACITY_FACTOR / E))
            xt = x.reshape(T, D)
            probs_full = jax.nn.softmax(xt @ Wr, axis=-1)
            topv, topi = jax.lax.top_k(probs_full, TOPK)
            topv = topv / jnp.sum(topv, axis=-1, keepdims=True)
            onehot = jax.nn.one_hot(topi, E, dtype=x.dtype)
            rank = jnp.cumsum(onehot, axis=0)
            keep = (rank <= capacity).astype(x.dtype) * onehot
            w = jnp.einsum('tk,tke->te', topv, keep)
            h = jax.nn.gelu(jnp.einsum('td,edf->etf', xt, W1) + b1[:, None, :], approximate=False)
            y = jnp.einsum('etf,efd->etd', h, W2) + b2[:, None, :]
            out = jnp.einsum('te,etd->td', w, y)
            return out.reshape(Bsz, Sl, D)
        return _moe(x, Wr, W1, b1, W2, b2)
    x = x + jnp.tanh(g_xattn[0]) * _L0_xattn_ref(_layernorm(x, axis=-1), ctx_1024, ctx_1024, L0_xattn_Wq, L0_xattn_Wk, L0_xattn_Wv, L0_xattn_Wo)
    x = x + jnp.tanh(g_ffn[0]) * _L0_ffn_ref(_layernorm(x, axis=-1), L0_ffn_Wr, L0_ffn_W1, L0_ffn_b1, L0_ffn_W2, L0_ffn_b2)
    return x

_drawn_inputs = setup_inputs


def setup_inputs(seed=0):
    import zlib

    import numpy as np

    out = dict(_drawn_inputs(seed))
    spreads = {'L0_ffn_b1': (0.0, 0.1), 'L0_ffn_b2': (0.0, 0.1)}
    factors = {}
    for name, (base, spread) in spreads.items():
        noise = np.random.default_rng([zlib.crc32(name.encode()), seed]).standard_normal(out[name].shape)
        drawn = base * np.exp(spread * noise) if base else spread * noise
        out[name] = jnp.asarray(drawn.astype(out[name].dtype))
    for name, factor in factors.items():
        out[name] = (out[name] * factor).astype(out[name].dtype)
    return out
```

```python
from contextlib import ExitStack

import concourse.bass as bass
from concourse import mybir

F32 = mybir.dt.float32
F32R = mybir.dt.float32r
BF16 = mybir.dt.bfloat16
U32 = mybir.dt.uint32
ALU = mybir.AluOpType
ACT = mybir.ActivationFunctionType
AX = mybir.AxisListType

P = 128
B, S, D = 2, 512, 128
C = 154
H, HD = 16, 8
T = B * S
NT = T // P
QT = S // P
C1 = C - P
CP = P + 32
Q1 = S - P
E, F = 8, 512
FC = F // P
TOPK = 2
CAP = max(1, int(T * 1.25 / E))
SLOTS = TOPK * CAP
ST = -(-SLOTS // P)
LAST = SLOTS - (ST - 1) * P
ROW = 132
SCALE = float(HD) ** -0.5
NEG = -1e30
EPS = 1e-5
FAR = 8192.0
VW = HD + 1


def groups_of_heads(qt):
    if qt == 0:
        return [(4 * n, 4, P) for n in range(4)]
    return [(0, 3, C), (3, 3, C), (6, 3, C), (9, 3, C), (12, 2, C), (14, 2, C)]


def build(nc, x, ctxT, gx, gf, wqT, wkT, wvT, woT, wr, w1, b1T, w2, b2, out):
    with ExitStack() as stack:
        def sb(name, shape, dt=F32):
            return stack.enter_context(nc.sbuf_tensor(name, shape, dt))

        def psum(name, shape, dt=F32):
            return stack.enter_context(nc.psum_tensor(name, shape, dt))

        def sem(name):
            return stack.enter_context(nc.semaphore(name))

        slots = nc.dram_tensor("slots", (E * SLOTS, ROW), F32, kind="Internal").ap()
        results = nc.dram_tensor("results", (TOPK * T, D), F32, kind="Internal").ap()

        X = sb("X", [P, NT, D])
        CT = sb("CT", [P, B, P + 4 * 32])
        WQ, WK, WV, WO = (sb(n, [P, D]) for n in ("WQ", "WK", "WV", "WO"))
        WR = sb("WR", [P, E])
        W1 = sb("W1", [P, E, F])
        B1 = sb("B1", [P, E, FC])
        W2 = sb("W2", [P, E, FC, D])
        B2 = sb("B2", [P, E, D])
        G = sb("G", [P, 2])
        zeros = sb("zeros", [P, D])
        slot0 = sb("slot0", [P, ROW])
        identf = sb("identf", [P, P])
        identb = sb("identb", [P, P], BF16)
        head_mask = sb("head_mask", [P, 4, 4])
        copy_mask = sb("copy_mask", [P, 4])
        pick_raw = sb("pick_raw", [P, 4, 4, 2])
        pick_row = sb("pick_row", [P, 4])
        pick0 = sb("pick0", [P, 4, P], BF16)
        pick1 = sb("pick1", [32, 4, 4, 32], BF16)
        mask_q = sb("mask_q", [P, 4, P], BF16)
        mask_k0 = sb("mask_k0", [P, P], BF16)
        mask_k1 = sb("mask_k1", [P, Q1], BF16)
        upto = sb("upto", [P, P], BF16)
        ones = sb("ones", [P, P], BF16)
        expert_no = sb("expert_no", [P, E])
        base = sb("base", [P, TOPK, E])
        choice_row = sb("choice_row", [P, ST])
        half = sb("half", [P, NT])
        stats = sb("stats", [P, NT, 6])
        mean_var = sb("mean_var", [P, NT, 2])
        rstd = sb("rstd", [P, NT])
        xn = sb("xn", [P, NT, D])
        xnT = sb("xnT", [P, B, S])
        qT = sb("qT", [P, B, S])
        qTr = sb("qTr", [P, B, S], F32R)
        kT = sb("kT", [P, B, CP])
        kTr = sb("kTr", [P, B, H, C], F32R)
        k0 = sb("k0", [P, B, 4, P])
        k1 = sb("k1", [P, B, 4, 4, 32])
        v0 = sb("v0", [P, B, H, VW])
        v1 = sb("v1", [P, B, 4, 4, VW])
        top = sb("top", [P, B, QT, H])
        top2 = sb("top2", [P, QT, 4, 2, H], BF16)
        topT = sb("topT", [P, B, S], BF16)
        p0 = sb("p0", [P, 2, 4, S])
        p1 = sb("p1", [P, 2, Q1])
        inv = sb("inv", [P, QT, 8])
        attn = sb("attn", [P, QT, 2, 8, HD])
        attnT = sb("attnT", [P, S])
        gate = sb("gate", [P, 2])
        x1 = sb("x1", [P, NT, D])
        rows = sb("rows", [P, NT, ROW])
        rowsT = sb("rowsT", [P, S])
        logits = sb("logits", [P, QT, E])
        best = sb("best", [P, QT, E])
        best_at = sb("best_at", [P, QT, E], U32)
        chosen = sb("chosen", [P, QT, TOPK])
        onehot = sb("onehot", [P, NT, TOPK, E], BF16)
        diff = sb("diff", [P, NT])
        ediff = sb("ediff", [P, NT])
        weight = sb("weight", [P, NT, TOPK])
        picked = sb("picked", [P, QT * TOPK, E])
        rank = sb("rank", [P, QT * TOPK])
        first = sb("first", [P, QT * TOPK])
        over = sb("over", [P, QT * TOPK])
        slot_of = sb("slot_of", [P, NT * TOPK], U32)
        xs = sb("xs", [P, E, ST, ROW])
        xsT = sb("xsT", [P, 2, SLOTS])
        hT = sb("hT", [P, 2, FC, SLOTS])
        y = sb("y", [P, E, ST, D])
        result_of = sb("result_of", [P, E, ST], U32)
        yk = sb("yk", [P, TOPK, NT, D])
        fin = sb("fin", [P, NT, D])

        sc = psum("sc", [P, 4, 512])
        sc1 = psum("sc1", [P, 512])
        av = psum("av", [P, 512])
        turn = [psum(f"turn{n}", [P, 512]) for n in range(2)]

        x_in = [sem(f"x_in{b}") for b in range(B)]
        ctx_in, wk_in, wv_in, wq_in, wo_in, small_in = (
            sem(n) for n in ("ctx_in", "wk_in", "wv_in", "wq_in", "wo_in", "small_in"))
        w_in = [sem(f"w_in{e}") for e in range(E)]
        pool_step = sem("pool_step")
        zero_ready = sem("zero_ready")
        ctx_pad = sem("ctx_pad")
        consts1, consts2, consts3 = sem("consts1"), sem("consts2"), sem("consts3")
        laid = sem("laid")
        vec_step = sem("vec_step")
        var_ready, rstd_ready, xn_ready = sem("var_ready"), sem("rstd_ready"), sem("xn_ready")
        kv_ps, kT_ready, v_ready = sem("kv_ps"), sem("kT_ready"), sem("v_ready")
        v_ones = sem("v_ones")
        copy_mask_ready = sem("copy_mask_ready")
        kTr_ready, k_ready = sem("kTr_ready"), sem("k_ready")
        xnT_ps, xnT_ready, q_ps, qT_ready, qTr_ready = (
            sem(n) for n in ("xnT_ps", "xnT_ready", "q_ps", "qT_ready", "qTr_ready"))
        turn_full, turn_free = sem("turn_full"), sem("turn_free")
        top_ready, pick_ready = sem("top_ready"), sem("pick_ready")
        sc_full, sc_free, pv_done = sem("sc_full"), sem("sc_free"), sem("pv_done")
        av_free = sem("av_free")
        gate_ready = sem("gate_ready")
        rows_ready = sem("rows_ready")
        onehot_ready, slot_ready = sem("onehot_ready"), sem("slot_ready")
        diff_ready, ediff_ready = sem("diff_ready"), sem("ediff_ready")
        sent = sem("sent")
        xs_in = [sem(f"xs_in{e}") for e in range(E)]
        xsT_ps, xsT_ready = sem("xsT_ps"), sem("xsT_ready")
        h_ps, h_ready = sem("h_ps"), sem("h_ready")
        y_ps, y_ready = sem("y_ps"), sem("y_ready")
        back = sem("back")
        yk_in = [sem(f"yk_in{n}") for n in range(4)]
        fin_ready, stored = sem("fin_ready"), sem("stored")

        x_d = x.rearrange("(n p) d -> p n d", p=P)
        out_d = out.rearrange("(n p) d -> p n d", p=P)
        res_d = results.rearrange("(k n p) d -> p k n d", p=P, k=TOPK)

        POST = 5
        NPIECES = 4
        maxima_todo = [(qt, *g) for qt in range(QT) for g in groups_of_heads(qt)]
        SHARE = -(-len(maxima_todo) // 4)

        block = stack.enter_context(nc.Block())

        @block.sync
        def _(sp):
            sp.dma_start(X[:, 0:QT, :], x_d[:, 0:QT, :]).then_inc(x_in[0], 16)
            sp.wait_ge(ctx_pad, 1)
            sp.dma_start(CT[:, :, 0:C], ctxT).then_inc(ctx_in, 16)
            for j in range(1, 4):
                sp.dma_start(CT[:, :, P + 32 * j:P + 32 * j + C1], ctxT[:, :, P:C]).then_inc(ctx_in, 16)
            sp.dma_start(X[:, QT:NT, :], x_d[:, QT:NT, :]).then_inc(x_in[1], 16)
            sp.wait_ge(zero_ready, 1)
            sp.dma_start(slots.rearrange("(p n) r -> p n r", p=P),
                         slot0[:, :].unsqueeze(1).to_broadcast([P, E * SLOTS // P, ROW])).then_inc(laid, 16)
            sp.dma_start(results.rearrange("(p n) d -> p n d", p=P),
                         zeros[:, :].unsqueeze(1).to_broadcast([P, TOPK * T // P, D])).then_inc(laid, 16)
            for e in range(E):
                sp.dma_start(W1[:, e, :], w1[e]).then_inc(w_in[e], 16)
                sp.dma_start(W2[:, e, :, :], w2[e].rearrange("(c p) d -> p c d", p=P)).then_inc(w_in[e], 16)
            sp.wait_ge(sent, 16 * NT * TOPK)
            for e in range(E):
                full = slots[e * SLOTS:e * SLOTS + (ST - 1) * P, :].rearrange("(n p) r -> p n r", p=P)
                sp.dma_start(xs[:, e, 0:ST - 1, :], full).then_inc(xs_in[e], 16)
                sp.dma_start(xs[0:LAST, e, ST - 1, :],
                             slots[e * SLOTS + (ST - 1) * P:(e + 1) * SLOTS, :]).then_inc(xs_in[e], 16)
            sp.wait_ge(back, 16 * E * ST)
            n = NT // NPIECES
            for c in range(NPIECES):
                for k in range(TOPK):
                    sp.dma_start(yk[:, k, n * c:n * c + n, :],
                                 res_d[:, k, n * c:n * c + n, :]).then_inc(yk_in[c], 16)
            for c in range(NPIECES):
                sp.wait_ge(fin_ready, n * (c + 1))
                sp.dma_start(out_d[:, n * c:n * c + n, :], fin[:, n * c:n * c + n, :]).then_inc(stored, 16)
            sp.wait_ge(stored, 16 * NPIECES)

        @block.gpsimd
        def _(pool):
            steps = [0]

            def step(ins):
                steps[0] += 1
                ins.then_inc(pool_step, 1)
                pool.wait_ge(pool_step, steps[0])

            pool.memset(CT[:, :, P:P + 4 * 32], 0.0).then_inc(ctx_pad, 1)
            pool.memset(zeros[:, :], 0.0)
            step(pool.memset(slot0[:, :], 0.0))
            step(pool.memset(slot0[:, D:D + 1], FAR))
            pool.memset(half[:, :], -0.5).then_inc(zero_ready, 1)
            pool.memset(identf[:, :], 0.0)
            step(pool.memset(head_mask[:, :, :], 1.0))
            step(pool.affine_select(out=identf[:, :], in_=identf[:, :], compare_op=ALU.not_equal, fill=1.0,
                                    base=0, pattern=[[-1, P]], channel_multiplier=1))
            step(pool.affine_select(out=head_mask[:, :, :], in_=head_mask[:, :, :], compare_op=ALU.is_ge,
                                    fill=0.0, base=0, pattern=[[-HD, 4], [-32, 4]], channel_multiplier=1))
            pool.affine_select(out=head_mask[:, :, :], in_=head_mask[:, :, :], compare_op=ALU.is_ge,
                               fill=0.0, base=HD - 1, pattern=[[HD, 4], [32, 4]],
                               channel_multiplier=-1).then_inc(consts1, 1)

            def root(b, n):
                pool.wait_ge(var_ready, n)
                nc.gpsimd.tensor_tensor(rstd[:, QT * b:QT * b + QT], mean_var[:, QT * b:QT * b + QT, 1],
                                        half[:, 0:QT], ALU.pow).then_inc(rstd_ready, 1)

            step(pool.memset(mask_q[:, :, :], 0.0))
            pool.affine_select(out=mask_q[:, :, :], in_=mask_q[:, :, :], compare_op=ALU.is_ge, fill=NEG,
                               base=0, pattern=[[0, 4], [-1, P]], channel_multiplier=1)
            step(pool.tensor_copy(identb[:, :], identf[:, :]))
            pool.memset(pick_raw[:, :, :, :], 0.0).then_inc(consts2, 1)
            root(0, 1)
            root(1, 2)
            step(pool.memset(v1[:, :, :, :, :], 0.0))
            step(pool.memset(v0[:, :, :, HD:VW], 1.0))
            for j in range(4):
                pool.memset(v1[32 * j:32 * j + 32, :, :, j, HD:VW], 1.0).then_inc(v_ones, 1)
                pool.wait_ge(v_ones, j + 1)
            step(pool.affine_select(out=pick_raw[:, :, :, :], in_=pick_raw[:, :, :, :],
                                    compare_op=ALU.not_equal, fill=-1.0, base=0,
                                    pattern=[[-4, 4], [-33, 4], [-16, 2]], channel_multiplier=1))
            pool.memset(mask_k0[:, :], 0.0)
            pool.memset(mask_k1[:, :], 0.0)
            step(pool.memset(pick1[:, :, :, :], 0.0))
            pool.affine_select(out=mask_k0[:, :], in_=mask_k0[:, :], compare_op=ALU.is_ge, fill=NEG,
                               base=0, pattern=[[1, P]], channel_multiplier=-1)
            for part in range(2):
                step(pool.affine_select(out=pick1[:, :, :, :], in_=pick1[:, :, :, :],
                                        compare_op=ALU.not_equal, fill=-1.0, base=-16 * part,
                                        pattern=[[-4, 4], [-1, 4], [0, 32]], channel_multiplier=1))
            for j in range(4):
                m = mask_k1[32 * j:32 * j + 32, :]
                step(pool.affine_select(out=m[:, 0:32], in_=m[:, 0:32], compare_op=ALU.is_ge, fill=NEG, base=0,
                                        pattern=[[1, 32]], channel_multiplier=-1))
                step(pool.affine_select(out=m, in_=m, compare_op=ALU.is_ge, fill=NEG, base=C1 - 1,
                                        pattern=[[0, Q1]], channel_multiplier=-1))
            pool.memset(ones[:, :], 1.0).then_inc(consts3, 1)
            pool.wait_ge(copy_mask_ready, 1)
            pool.wait_ge(kT_ready, 1)
            for b in range(B):
                pool.tensor_tensor(k0[:, b], kT[:, b, 0:P].unsqueeze(1).to_broadcast([P, 4, P]),
                                   copy_mask[:, :].unsqueeze(2).to_broadcast([P, 4, P]), ALU.mult)
                pool.tensor_tensor(k1[:, b].rearrange("p i j k -> p (i j) k"),
                                   kT[:, b, P:CP].unsqueeze(1).to_broadcast([P, H, 32]),
                                   head_mask[:, :, :].rearrange("p i j -> p (i j)").unsqueeze(2)
                                   .to_broadcast([P, H, 32]), ALU.mult).then_inc(k_ready, 1)
            step(pool.memset(upto[:, :], 1.0))
            pool.affine_select(out=upto[:, :], in_=upto[:, :], compare_op=ALU.is_ge, fill=0.0,
                               base=0, pattern=[[1, P]], channel_multiplier=-1)
            pool.iota(expert_no[:, :], pattern=[[1, E]], base=0, channel_multiplier=0,
                      allow_small_or_imprecise_dtypes=True)
            pool.iota(base[:, :, :], pattern=[[CAP, TOPK], [SLOTS, E]], base=-1, channel_multiplier=0,
                      allow_small_or_imprecise_dtypes=True)
            pool.memset(rows[:, :, D:ROW], 0.0)
            pool.memset(choice_row[:, 0:1], 0.0)
            step(pool.memset(choice_row[:, 1:ST], float(T)))
            step(pool.memset(choice_row[0:CAP - P, 1:2], 0.0))
            pool.iota(rows[:, :, D], pattern=[[P, NT]], base=0, channel_multiplier=1,
                      allow_small_or_imprecise_dtypes=True).then_inc(consts3, 1)

            pool.wait_ge(laid, 32)
            pool.wait_ge(consts3, 2)
            for b in range(B):
                root(b, 3 + b)
                pool.wait_ge(slot_ready, b + 1)
                for c in range(QT * TOPK * b, QT * TOPK * (b + 1)):
                    nc.gpsimd.indirect_dma_start(
                        out=slots, out_offset=bass.IndirectOffsetOnAxis(ap=slot_of[:, c:c + 1], axis=0),
                        in_=rows[:, c // TOPK, :], in_offset=None,
                        bounds_check=E * SLOTS - 1, oob_is_err=False).then_inc(sent, 16)
            for e in range(E):
                pool.wait_ge(y_ready, e + 1)
                for n in range(ST):
                    m = P if n < ST - 1 else LAST
                    nc.gpsimd.indirect_dma_start(
                        out=results, out_offset=bass.IndirectOffsetOnAxis(ap=result_of[0:m, e, n:n + 1], axis=0),
                        in_=y[0:m, e, n, :], in_offset=None,
                        bounds_check=TOPK * T - 1, oob_is_err=False).then_inc(back, 16)

        @block.scalar
        def _(act):
            act.dma_start(WK[:, :], wkT).then_inc(wk_in, 16)
            act.dma_start(WV[:, :], wvT).then_inc(wv_in, 16)
            act.dma_start(WQ[:, :], wqT).then_inc(wq_in, 16)
            act.dma_start(G[:, 0:1], gx.partition_broadcast(P)).then_inc(small_in, 16)
            act.dma_start(G[:, 1:2], gf.partition_broadcast(P)).then_inc(small_in, 16)
            act.dma_start(WR[:, :], wr).then_inc(small_in, 16)
            act.dma_start(B1[:, :, :], b1T).then_inc(small_in, 16)
            act.dma_start(WO[:, :], woT).then_inc(wo_in, 16)
            act.dma_start(B2[:, :, :], b2.partition_broadcast(P)).then_inc(wo_in, 16)
            act.wait_ge(small_in, 64)
            act.activation(gate[:, :], G[:, :], ACT.Tanh).then_inc(gate_ready, 1)

            act.wait_ge(kv_ps, 1)
            act.activation(kT[:, :, :], sc1[:, 0:B * CP], ACT.Copy).then_inc(kT_ready, 1)
            for b in range(B):
                act.wait_ge(xnT_ps, b + 1)
                act.activation(xnT[:, b, :], sc[:, b, :], ACT.Copy).then_inc(xnT_ready, 1)
                act.wait_ge(q_ps, b + 1)
                act.activation(qT[:, b, :], sc[:, 2 + b, :], ACT.Copy).then_inc(qT_ready, 1)
            act.wait_ge(kv_ps, 3)
            act.wait_ge(v_ones, 4)
            act.activation(v0[:, :, :, 0:HD], av[:, 0:B * D].rearrange("p (b h d) -> p b h d", b=B, h=H),
                           ACT.Copy).then_inc(v_ready, 1)
            last_keys = av[:, B * D:2 * B * D].rearrange("p (b j i d) -> p b i j d", b=B, j=4, i=4)
            for j in range(4):
                q = slice(32 * j, 32 * j + 32)
                act.activation(v1[q, :, :, j, 0:HD], last_keys[q, :, :, j, :], ACT.Copy).then_inc(v_ready, 1)

            for g in range(4 * B):
                if g >= 2:
                    act.wait_ge(pv_done, g - 1)
                for pair in range(2):
                    act.wait_ge(sc_full, 3 * g + pair + 1)
                    act.activation(p0[:, g % 2, 2 * pair:2 * pair + 2, :], sc[:, 2 * pair:2 * pair + 2, :],
                                   ACT.Exp, scale=SCALE).then_inc(sc_free, 1)
                act.wait_ge(sc_full, 3 * g + 3)
                act.activation(p1[:, g % 2, :], sc1[:, 0:Q1], ACT.Exp, scale=SCALE).then_inc(sc_free, 1)
            for b in range(B):
                act.wait_ge(diff_ready, b + 1)
                act.activation(ediff[:, QT * b:QT * b + QT], diff[:, QT * b:QT * b + QT],
                               ACT.Exp).then_inc(ediff_ready, 1)

            for e in range(E):
                if e >= 2:
                    act.wait_ge(y_ps, e - 1)
                for c in range(FC):
                    act.wait_ge(h_ps, FC * e + c + 1)
                    act.activation(hT[:, e % 2, c, :], sc[:, c, 0:SLOTS], ACT.Gelu,
                                   bias=B1[:, e, c:c + 1]).then_inc(h_ready, 1)

        @block.tensor
        def _(pe):
            uses = [0]

            def bank():
                n = uses[0]
                uses[0] += 1
                if n >= 2:
                    pe.wait_ge(turn_free, n - 1)
                return turn[n % 2]

            pe.wait_ge(ctx_in, 64)
            pe.wait_ge(wk_in, 16)
            pe.matmul(sc1[:, 0:B * CP], WK[:, :], CT[:, :, 0:CP], start=True, stop=True).then_inc(kv_ps, 1)
            pe.wait_ge(wv_in, 16)
            for b in range(B):
                mm = pe.matmul(av[:, b * D:b * D + D], CT[:, b, 0:P], WV[:, :], start=(b == 0), stop=True,
                               skip_group_check=True)
            mm.then_inc(kv_ps, 1)
            for b in range(B):
                mm = pe.matmul(av[:, (B + b) * D:(B + b) * D + D], CT[:, b, P:P + 128], WV[:, :],
                               start=False, stop=True, skip_group_check=True)
            mm.then_inc(kv_ps, 1)
            pe.wait_ge(wq_in, 16)
            pe.wait_ge(consts1, 1)
            for b in range(B):
                pe.wait_ge(xn_ready, b + 1)
                for t in range(QT):
                    mm = pe.transpose(sc[:, b, t * P:t * P + P], xn[:, QT * b + t, :], identf[:, :])
                mm.then_inc(xnT_ps, 1)
                pe.wait_ge(xnT_ready, b + 1)
                pe.matmul(sc[:, 2 + b, :], WQ[:, :], xnT[:, b, :], start=True, stop=True).then_inc(q_ps, 1)

            def maxima(b, todo):
                for qt, h0, nh, keys in todo:
                    ps = bank()
                    o = ps[:, 0:nh * keys].rearrange("p (h k) -> p h k", h=nh)
                    mm = pe.matmul(o, qTr[:, b, qt * P:qt * P + P], kTr[:, b, h0:h0 + nh, 0:keys],
                                   start=True, stop=(qt >= 2), skip_group_check=True)
                    if qt == 0:
                        mm = pe.matmul(o, identb[:, :], mask_q[:, 0:nh, :], start=False, stop=True,
                                       skip_group_check=True)
                    if qt == 1:
                        mm = pe.matmul(o[:, :, P:C], identb[:, :], mask_q[:, 0:nh, 0:C1], start=False,
                                       stop=True, skip_group_check=True)
                    mm.then_inc(turn_full, 1)

            use_of = {}

            def turn_maxima(b):
                pe.wait_ge(top_ready, b + 1)
                ps = bank()[:, 0:S // 2].bitcast(BF16)
                for t in range(QT):
                    mm = pe.transpose(ps[:, t * P:t * P + P],
                                      top2[:, t].rearrange("p c a h -> p (c a h)"), identb[:, :])
                mm.then_inc(turn_full, 1)
                use_of["maxima", b] = uses[0]

            def scores(g):
                b, i = divmod(g, 4)
                if g:
                    pe.wait_ge(sc_free, 3 * g - 1)
                for j in range(4):
                    q = slice(32 * j, 32 * j + 32)
                    pe.matmul(sc[:, j, :], k0[q, b, i, :], qT[q, b, :], start=True, stop=False,
                              skip_group_check=True)
                for j in range(4):
                    q = slice(32 * j, 32 * j + 32)
                    pe.matmul(sc[:, j, :], pick0[q, i, :], topT[q, b, :], start=False, stop=False,
                              skip_group_check=True)
                for j in range(4):
                    mm = pe.matmul(sc[:, j, 0:P], identb[:, :], mask_k0[:, :], start=False, stop=True,
                                   skip_group_check=True)
                    if j % 2:
                        mm.then_inc(sc_full, 1)
                if g:
                    pe.wait_ge(sc_free, 3 * g)
                pe.matmul(sc1[:, 0:Q1], k1[:, b, i].rearrange("p j k -> p (j k)"), qT[:, b, P:S],
                          start=True, stop=False, skip_group_check=True)
                pe.matmul(sc1[:, 0:Q1], pick1[:, i].rearrange("p j k -> p (j k)"), topT[0:32, b, P:S],
                          start=False, stop=False, skip_group_check=True)
                pe.matmul(sc1[:, 0:Q1], identb[:, :], mask_k1[:, :], start=False, stop=True,
                          skip_group_check=True).then_inc(sc_full, 1)

            def values(g):
                b, i = divmod(g, 4)
                pe.wait_ge(sc_free, 3 * g + 3)
                if i % 2 == 0 and g:
                    pe.wait_ge(av_free, g // 2)
                for t in range(QT):
                    at = (t * 2 + i % 2) * 4 * VW
                    for j in range(4):
                        mm = pe.matmul(av[:, at + j * VW:at + j * VW + VW], p0[:, g % 2, j, t * P:t * P + P],
                                       v0[:, b, 4 * j + i, :], start=(i % 2 == 0 and t == 0 and j == 0),
                                       stop=(t == 0), skip_group_check=True)
                    if t:
                        mm = pe.matmul(av[:, at:at + 4 * VW], p1[:, g % 2, (t - 1) * P:t * P],
                                       v1[:, b, i].rearrange("p j d -> p (j d)"), start=False, stop=True,
                                       skip_group_check=True)
                mm.then_inc(pv_done, 1)

            def post(b, n):
                if n == 0:
                    pe.wait_ge(av_free, 2 * b + 2)
                    ps = bank()
                    for t in range(QT):
                        mm = pe.transpose(ps[:, t * P:t * P + P],
                                          attn[:, t].rearrange("p a h d -> p (a h d)"), identf[:, :])
                if n == 1:
                    pe.wait_ge(turn_free, use_of[0, b])
                    pe.wait_ge(wo_in, 32)
                    ps = bank()
                    for t in range(QT):
                        mm = pe.matmul(ps[:, t * D:t * D + D], attnT[:, t * P:t * P + P], WO[:, :],
                                       start=(t == 0), stop=True, skip_group_check=True)
                if n == 2:
                    pe.wait_ge(rows_ready, b + 1)
                    ps = bank()
                    for t in range(QT):
                        mm = pe.transpose(ps[:, t * P:t * P + P], rows[:, QT * b + t, 0:D], identf[:, :])
                if n == 3:
                    pe.wait_ge(turn_free, use_of[2, b])
                    pe.wait_ge(small_in, 64)
                    ps = bank()
                    for t in range(QT):
                        mm = pe.matmul(ps[:, t * E:t * E + E], rowsT[:, t * P:t * P + P], WR[:, :],
                                       start=(t == 0), stop=True, skip_group_check=True)
                if n == 4:
                    pe.wait_ge(onehot_ready, b + 1)
                    pe.wait_ge(consts3, 2)
                    ps = bank()
                    w = TOPK * E
                    for t in range(QT):
                        at = QT * b + t
                        for s in range(at + 1):
                            mm = pe.matmul(ps[:, t * w:t * w + w], ones[:, :] if s < at else upto[:, :],
                                           onehot[:, s].rearrange("p k e -> p (k e)"),
                                           start=(t == 0 and s == 0), stop=(s == at), skip_group_check=True)
                mm.then_inc(turn_full, 1)
                use_of[n, b] = uses[0]

            pe.wait_ge(consts2, 1)
            pe.wait_ge(kTr_ready, 1)
            pe.wait_ge(qTr_ready, 1)
            maxima(0, maxima_todo)
            turn_maxima(0)
            pe.wait_ge(k_ready, 1)
            pe.wait_ge(pick_ready, 1)
            pe.wait_ge(consts3, 1)
            pe.wait_ge(v_ready, 5)
            pe.wait_ge(qT_ready, 2)
            pe.wait_ge(turn_free, use_of["maxima", 0])
            for g in range(4 * B):
                b, i = divmod(g, 4)
                if g == 4:
                    turn_maxima(1)
                    pe.wait_ge(turn_free, use_of["maxima", 1])
                    pe.wait_ge(k_ready, 2)
                scores(g)
                if g:
                    values(g - 1)
                if g == 0:
                    pe.wait_ge(kTr_ready, 2)
                    pe.wait_ge(qTr_ready, 2)
                if b == 0:
                    maxima(1, maxima_todo[SHARE * i:SHARE * (i + 1)])
                elif i:
                    post(0, i - 1)
            values(4 * B - 1)
            post(0, 3)
            post(1, 0)
            post(0, 4)
            for n in range(1, POST):
                post(1, n)

            def gather(e):
                ps = turn[e % 2]
                pe.wait_ge(xs_in[e], 32)
                if e == 0:
                    pe.wait_ge(turn_free, uses[0])
                if e > 1:
                    pe.wait_ge(xsT_ready, e - 1)
                for n in range(ST):
                    m = P if n < ST - 1 else LAST
                    mm = pe.transpose(ps[:, n * P:n * P + m], xs[0:m, e, n, 0:D], identf[0:m, 0:m])
                mm.then_inc(xsT_ps, 1)

            def up(e):
                pe.wait_ge(w_in[e], 32)
                pe.wait_ge(xsT_ready, e + 1)
                if e == 0:
                    pe.wait_ge(sc_free, 12 * B)
                for c in range(FC):
                    if e:
                        pe.wait_ge(h_ready, FC * (e - 1) + c + 1)
                    pe.matmul(sc[:, c, 0:SLOTS], W1[:, e, c * P:c * P + P], xsT[:, e % 2, :],
                              start=True, stop=True).then_inc(h_ps, 1)

            def down(e):
                ps = (sc1, av)[e % 2]
                if e >= 2:
                    pe.wait_ge(y_ready, e - 1)
                pe.wait_ge(h_ready, FC * e + FC)
                for n in range(ST):
                    m = P if n < ST - 1 else LAST
                    for c in range(FC):
                        mm = pe.matmul(ps[0:m, n * D:n * D + D], hT[:, e % 2, c, n * P:n * P + m],
                                       W2[:, e, c, :], start=(n == 0 and c == 0), stop=(c == FC - 1),
                                       skip_group_check=True)
                mm.then_inc(y_ps, 1)

            pe.wait_ge(av_free, 2 * B)
            gather(0)
            for e in range(E):
                up(e)
                if e + 1 < E:
                    gather(e + 1)
                if e:
                    down(e - 1)
            down(E - 1)

        @block.vector
        def _(dve):
            steps, uses, norms = [0], [0], [0]

            def step(ins):
                steps[0] += 1
                ins.then_inc(vec_step, 1)
                dve.wait_ge(vec_step, steps[0])

            def bank():
                uses[0] += 1
                dve.wait_ge(turn_full, uses[0])
                return turn[(uses[0] - 1) % 2]

            def layernorm(b, src, dst, ready):
                tiles = range(QT * b, QT * b + QT)
                for t in tiles:
                    last = dve.bn_stats(stats[:, t, :], src[:, t, :])
                step(last)
                for t in tiles:
                    last = dve.bn_aggr(mean_var[:, t, :], stats[:, t, :])
                step(last)
                v = mean_var[:, QT * b:QT * b + QT, 1]
                dve.tensor_scalar(v, v, EPS, None, ALU.add).then_inc(var_ready, 1)
                norms[0] += 1
                dve.wait_ge(rstd_ready, norms[0])
                for t in tiles:
                    last = dve.tensor_scalar(dst[:, t, 0:D], src[:, t, :], mean_var[:, t, 0:1],
                                             rstd[:, t:t + 1], ALU.subtract, ALU.mult)
                last.then_inc(ready, 1)

            def keys_for_max(b):
                dve.tensor_tensor(kTr[:, b], kT[:, b, 0:C].unsqueeze(1).to_broadcast([P, H, C]),
                                  head_mask[:, :, :].rearrange("p i j -> p (i j)").unsqueeze(2)
                                  .to_broadcast([P, H, C]), ALU.mult).then_inc(kTr_ready, 1)

            def maxima(b, todo):
                for qt, h0, nh, keys in todo:
                    ps = bank()
                    dve.tensor_reduce(top[:, b, qt, h0:h0 + nh],
                                      ps[:, 0:nh * keys].rearrange("p (h k) -> p h k", h=nh),
                                      AX.X, ALU.max).then_inc(turn_free, 1)

            def split_maxima(b):
                dve.wait_ge(turn_free, uses[0])
                full = top[:, b].unsqueeze(2).to_broadcast([P, QT, 4, H])
                step(dve.tensor_copy(top2[:, :, :, 0, :], full))
                dve.tensor_tensor(top2[:, :, :, 1, :], full, top2[:, :, :, 0, :],
                                  ALU.subtract).then_inc(top_ready, 1)

            def turned_maxima(b):
                ps = bank()
                dve.tensor_copy(topT[:, b, :], ps[:, 0:S // 2].bitcast(BF16)).then_inc(turn_free, 1)

            def normalise(n):
                dve.wait_ge(pv_done, 2 * n + 2)
                ps = av[:, 0:QT * 8 * VW].rearrange("p (t h d) -> p t h d", t=QT, h=8)
                step(dve.reciprocal(inv[:, :, :], ps[:, :, :, HD]))
                dve.tensor_tensor(attn[:, :, n % 2], ps[:, :, :, 0:HD],
                                  inv[:, :, :].unsqueeze(3).to_broadcast([P, QT, 8, HD]),
                                  ALU.mult).then_inc(av_free, 1)

            def copy_turned(dst):
                ps = bank()
                dve.tensor_copy(dst, ps[:, 0:S]).then_inc(turn_free, 1)

            def residual(b):
                tiles = slice(QT * b, QT * b + QT)
                ps = bank()
                dve.wait_ge(gate_ready, 1)
                dve.scalar_tensor_tensor(x1[:, tiles, :].rearrange("p t d -> p (t d)"), ps[:, :], gate[:, 0:1],
                                         X[:, tiles, :].rearrange("p t d -> p (t d)"),
                                         ALU.mult, ALU.add).then_inc(turn_free, 1)
                dve.wait_ge(turn_free, uses[0])
                layernorm(b, x1, rows, rows_ready)

            def choose(b):
                ps = bank()
                dve.tensor_copy(logits[:, :, :].rearrange("p t e -> p (t e)"),
                                ps[:, 0:QT * E]).then_inc(turn_free, 1)
                dve.wait_ge(turn_free, uses[0])
                for t in range(QT):
                    last = dve.max(best[:, t, :], logits[:, t, :])
                step(last)
                for t in range(QT):
                    last = dve.max_index(best_at[:, t, :], best[:, t, :], logits[:, t, :])
                step(last)
                step(dve.tensor_copy(chosen[:, :, :], best_at[:, :, 0:TOPK]))
                dve.wait_ge(consts3, 2)
                oh = onehot[:, QT * b:QT * b + QT].rearrange("p t k e -> p (t k) e")
                dve.tensor_tensor(oh, expert_no[:, :].unsqueeze(1).to_broadcast([P, QT * TOPK, E]),
                                  chosen[:, :, :].rearrange("p t k -> p (t k)").unsqueeze(2)
                                  .to_broadcast([P, QT * TOPK, E]), ALU.is_equal).then_inc(onehot_ready, 1)
                dve.tensor_tensor(diff[:, QT * b:QT * b + QT], best[:, :, 1], best[:, :, 0],
                                  ALU.subtract).then_inc(diff_ready, 1)
                dve.wait_ge(onehot_ready, b + 1)
                oh4 = oh.rearrange("p (t k) e -> p t (k e)", k=TOPK)
                step(dve.tensor_tensor(picked[:, :, :].rearrange("p (t k) e -> p t (k e)", k=TOPK), oh4,
                                       base[:, :, :].rearrange("p k e -> p (k e)").unsqueeze(1)
                                       .to_broadcast([P, QT, TOPK * E]), ALU.mult))
                step(dve.tensor_reduce(first[:, :], picked[:, :, :], AX.X, ALU.add))

            def place(b):
                ps = bank()
                oh = onehot[:, QT * b:QT * b + QT].rearrange("p t k e -> p (t k) e")
                dve.tensor_tensor(picked[:, :, :], ps[:, 0:QT * TOPK * E].rearrange("p (c e) -> p c e", e=E),
                                  oh, ALU.mult).then_inc(turn_free, 1)
                dve.wait_ge(turn_free, uses[0])
                step(dve.tensor_reduce(rank[:, :], picked[:, :, :], AX.X, ALU.add))
                dve.tensor_scalar(over[:, :], rank[:, :], float(CAP), FAR, ALU.is_gt, ALU.mult)
                step(dve.tensor_tensor(first[:, :], first[:, :], rank[:, :], ALU.add))
                dve.tensor_tensor(slot_of[:, QT * TOPK * b:QT * TOPK * (b + 1)], first[:, :], over[:, :],
                                  ALU.add).then_inc(slot_ready, 1)

            for b in range(B):
                dve.wait_ge(x_in[b], 16)
                layernorm(b, X, xn, xn_ready)
                if b == 0:
                    dve.wait_ge(consts1, 1)
                    dve.tensor_reduce(copy_mask[:, :], head_mask[:, :, :], AX.X,
                                      ALU.add).then_inc(copy_mask_ready, 1)
            dve.wait_ge(kT_ready, 1)
            keys_for_max(0)
            dve.wait_ge(qT_ready, 1)
            dve.tensor_copy(qTr[:, 0], qT[:, 0]).then_inc(qTr_ready, 1)
            maxima(0, maxima_todo)
            split_maxima(0)
            dve.wait_ge(consts3, 1)
            step(dve.tensor_reduce(pick_row[:, :], pick_raw[:, :, :, :], AX.XY, ALU.add))
            dve.tensor_copy(pick0[:, :, :], pick_row[:, :].unsqueeze(2)
                            .to_broadcast([P, 4, P])).then_inc(pick_ready, 1)
            turned_maxima(0)
            keys_for_max(1)
            dve.wait_ge(qT_ready, 2)
            dve.tensor_copy(qTr[:, 1], qT[:, 1]).then_inc(qTr_ready, 1)
            for i in range(4):
                if i == 2:
                    normalise(0)
                maxima(1, maxima_todo[SHARE * i:SHARE * (i + 1)])
            split_maxima(1)
            turned_maxima(1)
            normalise(1)
            copy_turned(attnT[:, :])
            normalise(2)
            residual(0)
            copy_turned(rowsT[:, :])
            normalise(3)
            choose(0)
            copy_turned(attnT[:, :])
            place(0)
            residual(1)
            copy_turned(rowsT[:, :])
            choose(1)
            place(1)

            dve.wait_ge(ediff_ready, B)
            step(dve.tensor_scalar(weight[:, :, 1], ediff[:, :], 1.0, None, ALU.add))
            step(dve.reciprocal(diff[:, :], weight[:, :, 1]))
            step(dve.tensor_scalar(weight[:, :, 0], diff[:, :], gate[:, 1:2], None, ALU.mult))
            step(dve.tensor_tensor(weight[:, :, 1], weight[:, :, 0], ediff[:, :], ALU.mult))

            def slots_turned(e):
                dve.wait_ge(xsT_ps, e + 1)
                if e >= 2:
                    dve.wait_ge(h_ps, FC * (e - 1))
                dve.tensor_copy(xsT[:, e % 2, :], turn[e % 2][:, 0:SLOTS]).then_inc(xsT_ready, 1)
                dve.tensor_tensor(result_of[:, e, 0:ST - 1], xs[:, e, 0:ST - 1, D], choice_row[:, 0:ST - 1],
                                  ALU.add)
                dve.tensor_tensor(result_of[0:LAST, e, ST - 1:ST], xs[0:LAST, e, ST - 1, D:D + 1],
                                  choice_row[0:LAST, ST - 1:ST], ALU.add)

            def results_out(e):
                ps = (sc1, av)[e % 2]
                dve.wait_ge(y_ps, e + 1)
                full = (ST - 1) * D
                dve.tensor_tensor(y[:, e, 0:ST - 1, :], ps[:, 0:full].rearrange("p (n d) -> p n d", d=D),
                                  B2[:, e, :].unsqueeze(1).to_broadcast([P, ST - 1, D]), ALU.add)
                dve.tensor_tensor(y[0:LAST, e, ST - 1, :], ps[0:LAST, full:full + D], B2[0:LAST, e, :],
                                  ALU.add).then_inc(y_ready, 1)

            dve.wait_ge(wo_in, 32)
            for e in range(E):
                slots_turned(e)
                if e >= 2:
                    results_out(e - 2)
            results_out(E - 2)
            results_out(E - 1)

            n = NT // NPIECES
            for c in range(NPIECES):
                dve.wait_ge(yk_in[c], 32)
                for k in range(TOPK):
                    for t in range(n * c, n * c + n):
                        last = dve.scalar_tensor_tensor(fin[:, t, :], yk[:, k, t, :], weight[:, t, k:k + 1],
                                                        (fin if k else x1)[:, t, :], ALU.mult, ALU.add)
                        if k:
                            last.then_inc(fin_ready, 1)
                    if not k:
                        step(last)


def kernel(x, ctx_1024, g_xattn, g_ffn, L0_xattn_Wq, L0_xattn_Wk, L0_xattn_Wv, L0_xattn_Wo,
           L0_ffn_Wr, L0_ffn_W1, L0_ffn_b1, L0_ffn_W2, L0_ffn_b2):
    import numpy as np
    from concourse import bacc
    from concourse.bass_utils import run_bass_kernel_spmd

    woT = np.transpose(np.reshape(L0_xattn_Wo, (D, 4, 4, HD)), (2, 1, 3, 0)).reshape(D, D)
    arrays = {
        "x": np.reshape(x, (T, D)),
        "ctxT": np.transpose(ctx_1024, (2, 0, 1)),
        "gx": g_xattn,
        "gf": g_ffn,
        "wqT": np.transpose(L0_xattn_Wq),
        "wkT": np.transpose(L0_xattn_Wk),
        "wvT": np.transpose(L0_xattn_Wv),
        "woT": woT,
        "wr": L0_ffn_Wr,
        "w1": L0_ffn_W1,
        "b1T": np.transpose(np.reshape(L0_ffn_b1, (E, FC, P)), (2, 0, 1)),
        "w2": L0_ffn_W2,
        "b2": L0_ffn_b2,
    }
    nc = bacc.Bacc("TRN2", target_bir_lowering=False, num_devices=1)
    args = []
    for name, a in arrays.items():
        arrays[name] = a = np.ascontiguousarray(a)
        args.append(nc.dram_tensor(name, a.shape, mybir.dt.from_np(a.dtype), kind="ExternalInput").ap())
    out = nc.dram_tensor("out", (T, D), F32, kind="ExternalOutput").ap()
    build(nc, *args, out)
    done = run_bass_kernel_spmd(nc, [arrays], core_ids=[0])
    return done.results[0]["out"].reshape(B, S, D)
```

```python
from contextlib import ExitStack

import concourse.bass as bass
from concourse import mybir

F32 = mybir.dt.float32
F32R = mybir.dt.float32r
BF16 = mybir.dt.bfloat16
F16 = mybir.dt.float16
U32 = mybir.dt.uint32
ALU = mybir.AluOpType
ACT = mybir.ActivationFunctionType
AX = mybir.AxisListType

P = 128
B, S, D = 2, 512, 128
C = 154
H, HD = 16, 8
T = B * S
NT = T // P
QT = S // P
C1 = C - P
CP = P + 32
Q1 = S - P
E, F = 8, 512
FC = F // P
TOPK = 2
CAP = max(1, int(T * 1.25 / E))
SLOTS = TOPK * CAP
ST = -(-SLOTS // P)
LAST = SLOTS - (ST - 1) * P
ROW = 132
SCALE = float(HD) ** -0.5
NEG = -1e30
EPS = 1e-5
FAR = 8192.0
OW = HD + 1
NG = 4 * B
VW = 32
SPLIT_FIRST = 6
PRODUCTS = ((0, 0), (0, 1), (1, 0))
PARTS = 3


def groups_of_heads(qt):
    if qt == 0:
        return [(4 * n, 4, P) for n in range(4)]
    return [(0, 3, C), (3, 3, C), (6, 3, C), (9, 3, C), (12, 2, C), (14, 2, C)]


def build(nc, x, ctxT, gx, gf, wqT, wkT, wvT, woT, wr, w1, b1T, w2, b2, out):
    with ExitStack() as stack:
        def sb(name, shape, dt=F32):
            return stack.enter_context(nc.sbuf_tensor(name, shape, dt))

        def psum(name, shape, dt=F32):
            return stack.enter_context(nc.psum_tensor(name, shape, dt))

        def sem(name):
            return stack.enter_context(nc.semaphore(name))

        slots = nc.dram_tensor("slots", (E * SLOTS, ROW), F32, kind="Internal").ap()
        results = nc.dram_tensor("results", (TOPK * T, D), F32, kind="Internal").ap()

        X = sb("X", [P, NT, D])
        CT = sb("CT", [P, B, P + 4 * 32])
        WQ, WK, WV, WO = (sb(n, [P, D]) for n in ("WQ", "WK", "WV", "WO"))
        WR = sb("WR", [P, E])
        W1 = sb("W1", [P, 2, F])
        B1 = sb("B1", [P, E, FC])
        W2 = sb("W2", [P, 2, FC, D])
        B2 = sb("B2", [P, E, D])
        G = sb("G", [P, 2])
        zeros = sb("zeros", [P, D])
        slot0 = sb("slot0", [P, ROW])
        identf = sb("identf", [P, P])
        identb = sb("identb", [P, P], BF16)
        head_mask = sb("head_mask", [P, 4, 4])
        block_mask = sb("block_mask", [P, 4])
        minus_raw = sb("minus_raw", [P, 4, 2])
        minus_one = sb("minus_one", [P, 1])
        pack_q = sb("pack_q", [P, 2, 4, 4, 4, HD], F32R)
        mask_q = sb("mask_q", [P, 4, P], BF16)
        mask_k0 = sb("mask_k0", [P, P], BF16)
        mask_k1 = sb("mask_k1", [P, 32], BF16)
        fold = sb("fold", [P, 4, OW])
        upto = sb("upto", [P, P], BF16)
        ones = sb("ones", [P, P], BF16)
        expert_no = sb("expert_no", [P, E])
        base = sb("base", [P, TOPK, E])
        choice_row = sb("choice_row", [P, ST])
        half = sb("half", [P, NT])
        stats = sb("stats", [P, NT, 6])
        mean_var = sb("mean_var", [P, NT, 2])
        rstd = sb("rstd", [P, NT])
        xn_all = sb("xn_all", [P, 2 * NT * D])
        xn = xn_all[:, 0:NT * D].rearrange("p (n d) -> p n d", n=NT)
        xnT = xn_all[:, NT * D:2 * NT * D].rearrange("p (b q) -> p b q", b=B)
        q_all = sb("q_all", [P, 2 * B * S], F32R)
        qT = q_all[:, :].rearrange("p (w b q) -> p w b q", w=2, b=B)
        kT = sb("kT", [P, B, CP])
        kT_part = sb("kT_part", [P, 2, B, CP], F32R)
        shared = sb("shared", [P, 2 * 2 * FC * ST * P], F32R)
        kTr = shared[:, 0:B * H * C].rearrange("p (b h k) -> p b h k", b=B, h=H)
        q_pack_all = sb("q_pack_all", [P, 4 * B * S], F32R)
        q_pack = q_pack_all[:, :].rearrange("p (i b q) -> p i b q", i=4, b=B)
        pack_k = q_pack_all[:, 0:2 * 4 * P].rearrange("p (w i j s d) -> p w i j s d", w=2, i=4, j=4, s=4)
        w1_all = sb("w1_all", [P, E * 2 * F], F32R)
        k_pack = w1_all[:, SPLIT_FIRST * 2 * F:SPLIT_FIRST * 2 * F + 4 * B * CP].rearrange(
            "p (i b k) -> p i b k", i=4, b=B)
        k1 = shared[:, B * H * C:B * H * C + B * 4 * P].rearrange("p (b i j k) -> p b i j k", b=B, i=4, j=4)
        vs = sb("vs", [P, 2 * B, H, PARTS, HD], BF16)
        v0 = sb("v0", [P, B, H, VW], BF16)
        v1 = sb("v1", [P, B, 4, 4, VW], BF16)
        top = sb("top", [P, B, QT, H])
        top2 = sb("top2", [P, QT, H, 4 * HD], BF16)
        p0_all = sb("p0_all", [P, 2 * 4 * S])
        p0 = p0_all[:, :].rearrange("p (t j q) -> p t j q", t=2, j=4)
        p1 = sb("p1", [P, 2, Q1])
        parts_all = sb("parts_all", [P, 2 * 2 * 4 * S], F16)
        p0_part = parts_all[:, :].rearrange("p (t w j q) -> p t w j q", t=2, w=2, j=4)
        pack_raw = parts_all[:, 0:2 * 2 * 2 * 4 * P].bitcast(F32).rearrange(
            "p (k w i j s d) -> p k w i j s d", k=2, w=2, i=4, j=4, s=4)
        p1_part = sb("p1_part", [P, 2, 2, Q1], F16)
        oT = sb("oT", [P, 2, S])
        v_rest = oT[:, :, :].rearrange("p w (b d) -> p w b d", b=2 * B)
        inv = sb("inv", [P, NG, QT, 4])
        attn = sb("attn", [P, QT, 4, 4, HD])
        attnT = CT[:, :, :].rearrange("p b k -> p (b k)")
        gate = sb("gate", [P, 2])
        x1 = X
        rows = sb("rows", [P, NT, ROW])
        rowsT = sb("rowsT", [P, S])
        logits = sb("logits", [P, QT, E])
        best = sb("best", [P, QT, E])
        best_at = sb("best_at", [P, QT, E], U32)
        chosen = sb("chosen", [P, QT, TOPK])
        onehot = sb("onehot", [P, NT, TOPK, E], BF16)
        diff = sb("diff", [P, NT])
        ediff = sb("ediff", [P, NT])
        weight = sb("weight", [P, NT, TOPK])
        picked = sb("picked", [P, QT * TOPK, E])
        rank = sb("rank", [P, QT * TOPK])
        first = sb("first", [P, QT * TOPK])
        over = sb("over", [P, QT * TOPK])
        slot_of = sb("slot_of", [P, NT * TOPK], U32)
        xs = parts_all[:, 0:2 * E * ST * ROW].bitcast(F32).rearrange("p (e n r) -> p e n r", e=E, n=ST)
        xsT = q_all[:, 0:2 * 2 * SLOTS].rearrange("p (t w s) -> p t w s", t=2, w=2)
        hT = p0_all[:, 0:2 * FC * SLOTS].rearrange("p (t c s) -> p t c s", t=2, c=FC)
        hT_part = shared[:, :].rearrange("p (t w c s) -> p t w c s", t=2, w=2, c=FC)
        w1_part = w1_all[:, :].rearrange("p (e w f) -> p e w f", e=E, w=2)
        w2_low = sb("w2_low", [P, SPLIT_FIRST, 2, FC, D], F32R)
        w2_high = q_pack_all[:, 0:(E - SPLIT_FIRST) * 2 * FC * D].rearrange(
            "p (e w c d) -> p e w c d", e=E - SPLIT_FIRST, w=2, c=FC)

        def w2_part(e):
            return w2_low[:, e] if e < SPLIT_FIRST else w2_high[:, e - SPLIT_FIRST]

        y = p1[:, :, :].rearrange("p t (n d) -> p t n d", d=D)
        result_of = sb("result_of", [P, E, ST], U32)
        yk = xn_all[:, :].rearrange("p (k n d) -> p k n d", k=TOPK, n=NT)
        fin = X

        sc = psum("sc", [P, 4, 512])
        sc1 = psum("sc1", [P, 512])
        av = psum("av", [P, 512])
        turn = [psum(f"turn{n}", [P, 512]) for n in range(2)]

        x_in = [sem(f"x_in{b}") for b in range(B)]
        ctx_in, ctx_rep_in, wk_in, wv_in, wq_in, wo_in, small_in = (
            sem(n) for n in ("ctx_in", "ctx_rep_in", "wk_in", "wv_in", "wq_in", "wo_in", "small_in"))
        w_in = [sem(f"w_in{e}") for e in range(E)]
        pool_step = sem("pool_step")
        zero_ready = sem("zero_ready")
        consts1, consts2, consts3 = sem("consts1"), sem("consts2"), sem("consts3")
        laid = sem("laid")
        vec_step = sem("vec_step")
        var_ready, rstd_ready, xn_ready = sem("var_ready"), sem("rstd_ready"), sem("xn_ready")
        kv_ps, kT_ready, v_copied, v_ready = (sem(n) for n in ("kv_ps", "kT_ready", "v_copied", "v_ready"))
        minus_ready, k_packed_ps, k_packed = sem("minus_ready"), sem("k_packed_ps"), sem("k_packed")
        q_packed_ps, q_packed = sem("q_packed_ps"), sem("q_packed")
        kT_split, kTr_first, kTr_ready, k_ready = sem("kT_split"), sem("kTr_first"), sem("kTr_ready"), sem("k_ready")
        xnT_ps, xnT_ready, q_ps, q_high, q_ready = (
            sem(n) for n in ("xnT_ps", "xnT_ready", "q_ps", "q_high", "q_ready"))
        turn_full, turn_free = sem("turn_full"), sem("turn_free")
        top_ready, pack_raw_ready, pack_ready = sem("top_ready"), sem("pack_raw_ready"), sem("pack_ready")
        sc_full, sc_free, pv_done = sem("sc_full"), sem("sc_free"), sem("pv_done")
        p_low = sem("p_low")
        oT_ready = sem("oT_ready")
        w_high, w_split = sem("w_high"), sem("w_split")
        cleared, v_part, v_left = sem("cleared"), sem("v_part"), sem("v_left")
        gate_ready = sem("gate_ready")
        rows_ready = sem("rows_ready")
        onehot_ready, slot_ready = sem("onehot_ready"), sem("slot_ready")
        diff_ready, ediff_ready = sem("diff_ready"), sem("ediff_ready")
        sent = sem("sent")
        xs_in = [sem(f"xs_in{e}") for e in range(E)]
        xsT_ps, xsT_ready = sem("xsT_ps"), sem("xsT_ready")
        h_ps, h_ready, h_split = sem("h_ps"), sem("h_ready"), sem("h_split")
        y_ps, y_ready = sem("y_ps"), sem("y_ready")
        back = sem("back")
        yk_in = [sem(f"yk_in{n}") for n in range(4)]
        fin_ready, stored = sem("fin_ready"), sem("stored")

        x_d = x.rearrange("(n p) d -> p n d", p=P)
        out_d = out.rearrange("(n p) d -> p n d", p=P)
        res_d = results.rearrange("(k n p) d -> p k n d", p=P, k=TOPK)

        POST = 5
        NPIECES = 4
        BESIDE = [(6, 0, 0), (7, 0, 2), (8, 0, 4)]
        BEHIND = [(6, 0, 1), (7, 0, 3)]
        maxima_todo = [[(qt, *h) for qt in range(QT) for h in groups_of_heads(qt) if h[0] // 4 == i]
                       for i in range(4)]
        FIRST_HEADS = 6

        def groups_ahead(g):
            return [n for n in ((1, 2) if g == 0 else (g + 2,)) if n < NG]

        pack_turn = [len(maxima_todo[0])]
        used = pack_turn[0] + 1
        for g in range(NG):
            for n in groups_ahead(g):
                used += len(maxima_todo[n % 4]) + (n == g + 2) * sum(when == g for when, _, _ in BESIDE)
                pack_turn.append(used)
                used += 1
            used += (g >= 2) + sum(when == g for when, _, _ in BEHIND)

        block = stack.enter_context(nc.Block())

        @block.sync
        def _(sp):
            sp.dma_start(X[:, 0:QT, :], x_d[:, 0:QT, :]).then_inc(x_in[0], 16)
            sp.dma_start(CT[:, :, 0:C], ctxT[:, :, 0:C]).then_inc(ctx_in, 16)
            sp.dma_start(CT[:, :, C:CP], ctxT[:, :, 0:CP - C]).then_inc(ctx_in, 16)
            sp.dma_start(X[:, QT:NT, :], x_d[:, QT:NT, :]).then_inc(x_in[1], 16)
            for j in range(1, 4):
                sp.dma_start(CT[:, :, P + 32 * j:P + 32 * j + C1], ctxT[:, :, P:C]).then_inc(ctx_rep_in, 16)
                sp.dma_start(CT[:, :, P + 32 * j + C1:P + 32 * j + 32],
                             ctxT[:, :, 0:CP - C]).then_inc(ctx_rep_in, 16)
            sp.wait_ge(zero_ready, 1)
            sp.dma_start(slots.rearrange("(p n) r -> p n r", p=P),
                         slot0[:, :].unsqueeze(1).to_broadcast([P, E * SLOTS // P, ROW])).then_inc(laid, 16)
            sp.dma_start(results.rearrange("(p n) d -> p n d", p=P),
                         zeros[:, :].unsqueeze(1).to_broadcast([P, TOPK * T // P, D])).then_inc(laid, 16)
            for e in range(E):
                if e >= 2:
                    sp.wait_ge(w_split, e - 1)
                sp.dma_start(W1[:, e % 2, :], w1[e]).then_inc(w_in[e], 16)
                sp.dma_start(W2[:, e % 2, :, :], w2[e].rearrange("(c p) d -> p c d", p=P)).then_inc(w_in[e], 16)
            sp.wait_ge(sent, 16 * NT * TOPK)
            for e in range(E):
                full = slots[e * SLOTS:e * SLOTS + (ST - 1) * P, :].rearrange("(n p) r -> p n r", p=P)
                sp.dma_start(xs[:, e, 0:ST - 1, :], full).then_inc(xs_in[e], 16)
                sp.dma_start(xs[0:LAST, e, ST - 1, :],
                             slots[e * SLOTS + (ST - 1) * P:(e + 1) * SLOTS, :]).then_inc(xs_in[e], 16)
            sp.wait_ge(back, 16 * E * ST)
            n = NT // NPIECES
            for c in range(NPIECES):
                for k in range(TOPK):
                    sp.dma_start(yk[:, k, n * c:n * c + n, :],
                                 res_d[:, k, n * c:n * c + n, :]).then_inc(yk_in[c], 16)
            for c in range(NPIECES):
                sp.wait_ge(fin_ready, n * (c + 1))
                sp.dma_start(out_d[:, n * c:n * c + n, :], fin[:, n * c:n * c + n, :]).then_inc(stored, 16)
            sp.wait_ge(stored, 16 * NPIECES)

        @block.gpsimd
        def _(pool):
            steps = [0]

            def step(ins):
                steps[0] += 1
                ins.then_inc(pool_step, 1)
                pool.wait_ge(pool_step, steps[0])

            pool.memset(zeros[:, :], 0.0)
            step(pool.memset(slot0[:, :], 0.0))
            step(pool.memset(slot0[:, D:D + 1], FAR))
            pool.memset(half[:, :], -0.5).then_inc(zero_ready, 1)
            pool.memset(identf[:, :], 0.0)
            step(pool.memset(head_mask[:, :, :], 1.0))
            step(pool.affine_select(out=identf[:, :], in_=identf[:, :], compare_op=ALU.not_equal, fill=1.0,
                                    base=0, pattern=[[-1, P]], channel_multiplier=1))
            step(pool.affine_select(out=head_mask[:, :, :], in_=head_mask[:, :, :], compare_op=ALU.is_ge,
                                    fill=0.0, base=0, pattern=[[-HD, 4], [-32, 4]], channel_multiplier=1))
            pool.affine_select(out=head_mask[:, :, :], in_=head_mask[:, :, :], compare_op=ALU.is_ge,
                               fill=0.0, base=HD - 1, pattern=[[HD, 4], [32, 4]],
                               channel_multiplier=-1).then_inc(consts1, 1)
            step(pool.memset(minus_raw[:, :, :], 0.0))
            step(pool.affine_select(out=minus_raw[:, :, :], in_=minus_raw[:, :, :], compare_op=ALU.not_equal,
                                    fill=-1.0, base=-3 * HD, pattern=[[-32, 4], [-1, 2]],
                                    channel_multiplier=1))

            def packing(dst, part_of):
                for pair, part in enumerate(part_of):
                    m = dst[:, part, :, :, pair, :]
                    last = pool.affine_select(out=m, in_=m, compare_op=ALU.not_equal, fill=1.0, base=0,
                                              pattern=[[-HD, 4], [-32, 4], [-1, HD]], channel_multiplier=1)
                return last

            def root(b, n):
                pool.wait_ge(var_ready, n)
                nc.gpsimd.tensor_tensor(rstd[:, QT * b:QT * b + QT], mean_var[:, QT * b:QT * b + QT, 1],
                                        half[:, 0:QT], ALU.pow).then_inc(rstd_ready, 1)

            step(pool.memset(mask_q[:, :, :], 0.0))
            pool.affine_select(out=mask_q[:, :, :], in_=mask_q[:, :, :], compare_op=ALU.is_ge, fill=NEG,
                               base=0, pattern=[[0, 4], [-1, P]], channel_multiplier=1)
            pool.tensor_copy(identb[:, :], identf[:, :]).then_inc(consts2, 1)
            root(0, 1)
            pool.wait_ge(cleared, 1)
            packing(pack_raw[:, 0], [kp for kp, qp in PRODUCTS]).then_inc(pack_raw_ready, 1)
            packing(pack_raw[:, 1], [qp for kp, qp in PRODUCTS]).then_inc(pack_raw_ready, 1)
            root(1, 2)
            pool.wait_ge(cleared, 2)
            step(pool.memset(v0[:, :, :, PARTS * HD:PARTS * HD + 1], 1.0))
            for j in range(4):
                step(pool.memset(v1[32 * j:32 * j + C1, :, :, j, PARTS * HD:PARTS * HD + 1], 1.0))
            step(pool.memset(block_mask[:, :], 1.0))
            step(pool.affine_select(out=block_mask[:, :], in_=block_mask[:, :], compare_op=ALU.is_ge,
                                    fill=0.0, base=0, pattern=[[-32, 4]], channel_multiplier=1))
            step(pool.affine_select(out=block_mask[:, :], in_=block_mask[:, :], compare_op=ALU.is_ge,
                                    fill=0.0, base=31, pattern=[[32, 4]], channel_multiplier=-1))

            def keys_for_max(b, h0):
                pool.tensor_tensor(kTr[:, b, h0:H],
                                   kT_part[:, 0, b, 0:C].unsqueeze(1).to_broadcast([P, H - h0, C]),
                                   head_mask[:, :, :].rearrange("p i j -> p (i j)")[:, h0:H].unsqueeze(2)
                                   .to_broadcast([P, H - h0, C]), ALU.mult).then_inc(kTr_ready, 1)

            pool.wait_ge(kT_split, 1)
            keys_for_max(0, FIRST_HEADS)
            pool.memset(mask_k1[:, :], 0.0)
            step(pool.memset(mask_k0[:, :], 0.0))
            pool.affine_select(out=mask_k0[:, :], in_=mask_k0[:, :], compare_op=ALU.is_ge, fill=NEG,
                               base=0, pattern=[[1, P]], channel_multiplier=-1)
            for j in range(4):
                m = mask_k1[32 * j:32 * j + 32, :]
                step(pool.affine_select(out=m, in_=m, compare_op=ALU.is_ge, fill=NEG, base=0,
                                        pattern=[[1, 32]], channel_multiplier=-1))
            step(pool.memset(fold[:, :, :], 0.0))
            for part in range(PARTS + 1):
                cols = fold[:, :, 0:HD] if part < PARTS else fold[:, :, HD:OW]
                step(pool.affine_select(out=cols, in_=cols, compare_op=ALU.not_equal, fill=1.0,
                                        base=-HD * part, pattern=[[-32, 4], [-1, HD if part < PARTS else 1]],
                                        channel_multiplier=1))
            pool.memset(ones[:, :], 1.0).then_inc(consts3, 1)
            pool.wait_ge(k_packed, 4)
            for b in range(B):
                pool.tensor_tensor(k1[:, b], k_pack[:, :, b, P:CP].unsqueeze(2).to_broadcast([P, 4, 4, 32]),
                                   block_mask[:, :].unsqueeze(1).unsqueeze(3).to_broadcast([P, 4, 4, 32]),
                                   ALU.mult).then_inc(k_ready, 1)
            for part in range(PARTS - 1):
                pool.wait_ge(v_part, part + 1)
                pool.tensor_tensor(v_rest[:, part % 2].rearrange("p b (h d) -> p b h d", h=H),
                                   v_rest[:, (part + 1) % 2].rearrange("p b (h d) -> p b h d", h=H),
                                   vs[:, :, :, part, :], ALU.subtract).then_inc(v_left, 1)
            keys_for_max(1, 0)
            step(pool.memset(upto[:, :], 1.0))
            pool.affine_select(out=upto[:, :], in_=upto[:, :], compare_op=ALU.is_ge, fill=0.0,
                               base=0, pattern=[[1, P]], channel_multiplier=-1)
            pool.iota(expert_no[:, :], pattern=[[1, E]], base=0, channel_multiplier=0,
                      allow_small_or_imprecise_dtypes=True)
            pool.iota(base[:, :, :], pattern=[[CAP, TOPK], [SLOTS, E]], base=-1, channel_multiplier=0,
                      allow_small_or_imprecise_dtypes=True)
            pool.memset(rows[:, :, D:ROW], 0.0)
            pool.memset(choice_row[:, 0:1], 0.0)
            step(pool.memset(choice_row[:, 1:ST], float(T)))
            step(pool.memset(choice_row[0:CAP - P, 1:2], 0.0))
            pool.iota(rows[:, :, D], pattern=[[P, NT]], base=0, channel_multiplier=1,
                      allow_small_or_imprecise_dtypes=True).then_inc(consts3, 1)

            def split_weights(e):
                pool.wait_ge(w_high, e + 1)
                for w, part in ((W1[:, e % 2], w1_part[:, e]), (W2[:, e % 2], w2_part(e))):
                    last = pool.tensor_tensor(part[:, 1], w, part[:, 0], ALU.subtract)
                last.then_inc(w_split, 1)

            for e in range(SPLIT_FIRST):
                split_weights(e)
            pool.wait_ge(laid, 32)
            pool.wait_ge(consts3, 2)
            for b in range(B):
                root(b, 3 + b)
                pool.wait_ge(slot_ready, b + 1)
                for c in range(QT * TOPK * b, QT * TOPK * (b + 1)):
                    nc.gpsimd.indirect_dma_start(
                        out=slots, out_offset=bass.IndirectOffsetOnAxis(ap=slot_of[:, c:c + 1], axis=0),
                        in_=rows[:, c // TOPK, :], in_offset=None,
                        bounds_check=E * SLOTS - 1, oob_is_err=False).then_inc(sent, 16)
            for e in range(SPLIT_FIRST, E):
                split_weights(e)
            for e in range(E):
                pool.wait_ge(y_ready, e + 1)
                if e >= 1:
                    pool.wait_ge(back, 16 * ST * e)
                for n in range(ST):
                    m = P if n < ST - 1 else LAST
                    nc.gpsimd.indirect_dma_start(
                        out=results, out_offset=bass.IndirectOffsetOnAxis(ap=result_of[0:m, e, n:n + 1], axis=0),
                        in_=y[0:m, e % 2, n, :], in_offset=None,
                        bounds_check=TOPK * T - 1, oob_is_err=False).then_inc(back, 16)

        @block.scalar
        def _(act):
            act.dma_start(WK[:, :], wkT).then_inc(wk_in, 16)
            act.dma_start(WV[:, :], wvT).then_inc(wv_in, 16)
            act.dma_start(WQ[:, :], wqT).then_inc(wq_in, 16)
            act.dma_start(G[:, 0:1], gx.partition_broadcast(P)).then_inc(small_in, 16)
            act.dma_start(G[:, 1:2], gf.partition_broadcast(P)).then_inc(small_in, 16)
            act.dma_start(WR[:, :], wr).then_inc(small_in, 16)
            act.dma_start(B1[:, :, :], b1T).then_inc(small_in, 16)
            act.dma_start(WO[:, :], woT).then_inc(wo_in, 16)
            act.dma_start(B2[:, :, :], b2.partition_broadcast(P)).then_inc(wo_in, 16)
            act.wait_ge(kv_ps, 1)
            act.activation(kT[:, :, :], sc1[:, 0:B * CP], ACT.Copy).then_inc(kT_ready, 1)
            for b in range(B):
                act.wait_ge(xnT_ps, b + 1)
                act.activation(xnT[:, b, :], sc[:, b, :], ACT.Copy).then_inc(xnT_ready, 1)
                act.wait_ge(q_ps, b + 1)
                act.activation(qT[:, 0, b, :], sc[:, 2 + b, :], ACT.Copy).then_inc(q_high, 1)
            for n, dst in enumerate((pack_k, pack_q)):
                act.wait_ge(pack_raw_ready, n + 1)
                act.activation(dst[:, :, :, :, :, :], pack_raw[:, n], ACT.Copy).then_inc(pack_ready, 1)
            act.wait_ge(minus_ready, 1)
            for i in range(4):
                act.wait_ge(k_packed_ps, i + 1)
                act.activation(k_pack[:, i], (sc1, av)[i % 2][:, 0:B * CP].rearrange("p (b k) -> p b k", b=B),
                               ACT.Identity, bias=minus_one[:, :]).then_inc(k_packed, 1)
            act.wait_ge(kv_ps, 2)
            act.activation(v_rest[:, 1].rearrange("p b d -> p (b d)"), turn[1][:, :], ACT.Copy).then_inc(v_copied, 1)
            for part in range(PARTS):
                if part == 0:
                    act.wait_ge(v_copied, 1)
                else:
                    act.wait_ge(v_left, part)
                act.activation(vs[:, :, :, part, :],
                               v_rest[:, (part + 1) % 2].rearrange("p b (h d) -> p b h d", h=H),
                               ACT.Copy).then_inc(v_part, 1)
            act.wait_ge(v_part, PARTS)
            act.wait_ge(consts3, 1)
            for b in range(B):
                act.activation(v0[:, b, :, 0:PARTS * HD], vs[:, b].rearrange("p h s d -> p h (s d)"),
                               ACT.Copy).then_inc(v_ready, 1)
            for b in range(B):
                last_keys = vs[:, B + b].rearrange("p (j i) s d -> p i j (s d)", i=4)
                for j in range(4):
                    q = slice(32 * j, 32 * j + C1)
                    act.activation(v1[q, b, :, j, 0:PARTS * HD], last_keys[q, :, j, :],
                                   ACT.Copy).then_inc(v_ready, 1)

            def pack(g):
                act.wait_ge(q_packed_ps, g + 1)
                act.activation(q_pack[:, g % 4, g // 4, :], turn[pack_turn[g] % 2][:, :],
                               ACT.Copy).then_inc(q_packed, 1)

            def high_weights(e):
                act.wait_ge(w_in[e], 32)
                act.activation(w1_part[:, e, 0], W1[:, e % 2], ACT.Copy)
                act.activation(w2_part(e)[:, 0], W2[:, e % 2], ACT.Copy).then_inc(w_high, 1)

            for e in range(2):
                high_weights(e)
            pack(0)
            act.wait_ge(small_in, 64)
            act.activation(gate[:, :], G[:, :], ACT.Tanh).then_inc(gate_ready, 1)
            for g in range(NG):
                t = g % 2
                if g >= 2:
                    act.wait_ge(p_low, 2 * g - 2)
                    act.wait_ge(pv_done, g - 1)
                for pair in range(2):
                    heads = slice(2 * pair, 2 * pair + 2)
                    act.wait_ge(sc_full, 3 * g + pair + 1)
                    act.activation(p0[:, t, heads, :], sc[:, heads, :], ACT.Exp, scale=SCALE)
                    act.activation(p0_part[:, t, 0, heads, :], sc[:, heads, :], ACT.Exp,
                                   scale=SCALE).then_inc(sc_free, 1)
                act.wait_ge(sc_full, 3 * g + 3)
                act.activation(p1[:, t, :], sc1[:, 0:Q1], ACT.Exp, scale=SCALE)
                act.activation(p1_part[:, t, 0, :], sc1[:, 0:Q1], ACT.Exp, scale=SCALE).then_inc(sc_free, 1)
                for n in groups_ahead(g):
                    pack(n)
                if 2 + g < SPLIT_FIRST:
                    high_weights(2 + g)
            act.wait_ge(sc_full, 3 * NG)
            for e in range(SPLIT_FIRST, E):
                high_weights(e)

            for b in range(B):
                act.wait_ge(diff_ready, b + 1)
                act.activation(ediff[:, QT * b:QT * b + QT], diff[:, QT * b:QT * b + QT],
                               ACT.Exp).then_inc(ediff_ready, 1)

            for e in range(E):
                if e >= 2:
                    act.wait_ge(h_split, 2 * e - 2)
                for c in range(FC):
                    act.wait_ge(h_ps, FC * e + c + 1)
                    act.activation(hT[:, e % 2, c, :], sc[:, c, 0:SLOTS], ACT.Gelu,
                                   bias=B1[:, e, c:c + 1]).then_inc(h_ready, 1)

        @block.tensor
        def _(pe):
            uses, full = [0], [0]
            occupied = [None, None]

            def bank(reader=None):
                n = uses[0] % 2
                uses[0] += 1
                if occupied[n]:
                    pe.wait_ge(*occupied[n])
                if reader is None:
                    full[0] += 1
                    reader = (turn_free, full[0])
                occupied[n] = reader
                return turn[n]

            pe.wait_ge(ctx_in, 32)
            pe.wait_ge(wk_in, 16)
            pe.matmul(sc1[:, 0:B * CP], WK[:, :], CT[:, :, 0:CP], start=True, stop=True).then_inc(kv_ps, 1)
            pe.wait_ge(wq_in, 16)
            pe.wait_ge(consts1, 1)
            for b in range(B):
                pe.wait_ge(xn_ready, b + 1)
                for t in range(QT):
                    mm = pe.transpose(sc[:, b, t * P:t * P + P], xn[:, QT * b + t, :], identf[:, :])
                mm.then_inc(xnT_ps, 1)
                pe.wait_ge(xnT_ready, b + 1)
                pe.matmul(sc[:, 2 + b, :], WQ[:, :], xnT[:, b, :], start=True, stop=True).then_inc(q_ps, 1)
            pe.wait_ge(kT_split, 1)
            pe.wait_ge(pack_ready, 1)
            for i in range(4):
                if i >= 2:
                    pe.wait_ge(k_packed, i - 1)
                for part in range(2):
                    mm = pe.matmul((sc1, av)[i % 2][:, 0:B * CP],
                                   pack_k[:, part, i].rearrange("p j s d -> p (j s d)"),
                                   kT_part[:, part].rearrange("p b k -> p (b k)"), start=(part == 0),
                                   stop=(part == 1))
                mm.then_inc(k_packed_ps, 1)
            pe.wait_ge(wv_in, 16)
            pe.wait_ge(ctx_rep_in, 16 * 6)
            for b in range(B):
                pe.matmul(turn[1][:, b * D:b * D + D], CT[:, b, 0:P], WV[:, :], start=(b == 0), stop=True,
                          skip_group_check=True)
            for b in range(B):
                mm = pe.matmul(turn[1][:, (B + b) * D:(B + b) * D + D], CT[:, b, P:P + 128], WV[:, :],
                               start=False, stop=True, skip_group_check=True)
            mm.then_inc(kv_ps, 1)

            def maxima(b, todo):
                for qt, h0, nh, keys in todo:
                    ps = bank()
                    o = ps[:, 0:nh * keys].rearrange("p (h k) -> p h k", h=nh)
                    mm = pe.matmul(o, qT[:, 0, b, qt * P:qt * P + P], kTr[:, b, h0:h0 + nh, 0:keys],
                                   start=True, stop=(qt >= 2), skip_group_check=True)
                    if qt == 0:
                        mm = pe.matmul(o, identb[:, :], mask_q[:, 0:nh, :], start=False, stop=True,
                                       skip_group_check=True)
                    if qt == 1:
                        mm = pe.matmul(o[:, :, P:C], identb[:, :], mask_q[:, 0:nh, 0:C1], start=False,
                                       stop=True, skip_group_check=True)
                    mm.then_inc(turn_full, 1)

            use_of = {}

            def pack_dims(b, i, ps):
                for part in range(2):
                    pe.matmul(ps, pack_q[:, part, i].rearrange("p j s d -> p (j s d)"), qT[:, part, b, :],
                              start=(part == 0), stop=False, skip_group_check=True)

            def pack_maxima(i, ps):
                for t in range(QT):
                    mm = pe.matmul(ps[:, t * P:t * P + P],
                                   top2[:, t, 4 * i:4 * i + 4, :].rearrange("p j s -> p (j s)"), identb[:, :],
                                   start=False, stop=True, skip_group_check=True)
                return mm

            def scores(g):
                b, i = divmod(g, 4)
                pe.wait_ge(q_packed, g + 1)
                for j in range(4):
                    if g and j % 2 == 0:
                        pe.wait_ge(sc_free, 3 * g - 2 + j // 2)
                    q = slice(32 * j, 32 * j + 32)
                    pe.matmul(sc[:, j, :], k_pack[q, i, b, 0:P], q_pack[q, i, b, :], start=True, stop=False,
                              skip_group_check=True)
                    mm = pe.matmul(sc[:, j, 0:P], identb[:, :], mask_k0[:, :], start=False, stop=True,
                                   skip_group_check=True)
                    if j % 2:
                        mm.then_inc(sc_full, 1)
                if g:
                    pe.wait_ge(sc_free, 3 * g)
                pe.matmul(sc1[:, 0:Q1], k1[:, b, i].rearrange("p j k -> p (j k)"), q_pack[:, i, b, P:S],
                          start=True, stop=False, skip_group_check=True)
                pe.matmul(sc1[:, 0:32], identb[:, :], mask_k1[:, :], start=False, stop=True,
                          skip_group_check=True).then_inc(sc_full, 1)

            def values(g):
                b, i = divmod(g, 4)
                if g:
                    pe.wait_ge(oT_ready, g)
                for part in range(2):
                    if part == 0:
                        pe.wait_ge(sc_free, 3 * g + 3)
                    else:
                        pe.wait_ge(p_low, 2 * g + 2)
                    for j in range(4):
                        pe.matmul(av[32 * j:32 * j + VW, :], v0[:, b, 4 * j + i, :],
                                  p0_part[:, g % 2, part, j, :], start=(part == 0), stop=False,
                                  skip_group_check=True)
                for part in range(2):
                    mm = pe.matmul(av[:, P:S], v1[:, b, i].rearrange("p j d -> p (j d)"),
                                   p1_part[:, g % 2, part, :], start=False, stop=(part == 1),
                                   skip_group_check=True)
                mm.then_inc(pv_done, 1)

            def fold_parts(g):
                pe.wait_ge(oT_ready, g + 1)
                ps = bank()
                w = 4 * OW
                for t in range(QT):
                    mm = pe.matmul(ps[:, t * w:t * w + w], oT[:, g % 2, t * P:t * P + P],
                                   fold[:, :, :].rearrange("p j d -> p (j d)"), start=(t == 0), stop=True,
                                   skip_group_check=True)
                mm.then_inc(turn_full, 1)
                use_of["fold", g] = full[0]

            def post(b, n):
                if n == 0:
                    pe.wait_ge(turn_free, use_of["fold", 4 * b + 3])
                    ps = bank()
                    for t in range(QT):
                        mm = pe.transpose(ps[:, t * P:t * P + P],
                                          attn[:, t].rearrange("p i j d -> p (i j d)"), identf[:, :])
                if n == 1:
                    pe.wait_ge(turn_free, use_of[0, b])
                    pe.wait_ge(wo_in, 32)
                    ps = bank()
                    for t in range(QT):
                        mm = pe.matmul(ps[:, t * D:t * D + D], attnT[:, t * P:t * P + P], WO[:, :],
                                       start=(t == 0), stop=True, skip_group_check=True)
                if n == 2:
                    pe.wait_ge(rows_ready, b + 1)
                    ps = bank()
                    for t in range(QT):
                        mm = pe.transpose(ps[:, t * P:t * P + P], rows[:, QT * b + t, 0:D], identf[:, :])
                if n == 3:
                    pe.wait_ge(turn_free, use_of[2, b])
                    pe.wait_ge(small_in, 64)
                    ps = bank()
                    for t in range(QT):
                        mm = pe.matmul(ps[:, t * E:t * E + E], rowsT[:, t * P:t * P + P], WR[:, :],
                                       start=(t == 0), stop=True, skip_group_check=True)
                if n == 4:
                    pe.wait_ge(onehot_ready, b + 1)
                    pe.wait_ge(consts3, 2)
                    ps = bank()
                    w = TOPK * E
                    for t in range(QT):
                        at = QT * b + t
                        for s in range(at + 1):
                            mm = pe.matmul(ps[:, t * w:t * w + w], ones[:, :] if s < at else upto[:, :],
                                           onehot[:, s].rearrange("p k e -> p (k e)"),
                                           start=(t == 0 and s == 0), stop=(s == at), skip_group_check=True)
                mm.then_inc(turn_full, 1)
                use_of[n, b] = full[0]


            def pack(g):
                b, i = divmod(g, 4)
                ps = bank((q_packed, g + 1))
                pack_dims(b, i, ps[:, :])
                pe.wait_ge(top_ready, g + 1)
                pack_maxima(i, ps).then_inc(q_packed_ps, 1)

            pe.wait_ge(consts2, 1)
            pe.wait_ge(v_copied, 1)
            pe.wait_ge(kTr_first, 1)
            maxima(0, maxima_todo[0])
            pe.wait_ge(pack_ready, 2)
            pe.wait_ge(q_ready, 2)
            pack(0)
            pe.wait_ge(k_ready, 2)
            pe.wait_ge(consts3, 1)
            for g in range(NG + 2):
                if g < NG:
                    scores(g)
                for n in groups_ahead(g):
                    if n in (1, 4):
                        pe.wait_ge(kTr_ready, 1 if n == 1 else 2)
                    maxima(n // 4, maxima_todo[n % 4])
                    if n != g + 2:
                        pack(n)
                for when, b, n in BESIDE:
                    if when == g:
                        post(b, n)
                if g == 1:
                    pe.wait_ge(v_ready, 5 * B)
                if 1 <= g <= NG:
                    values(g - 1)
                if g + 2 < NG:
                    pack(g + 2)
                if g >= 2:
                    fold_parts(g - 2)
                for when, b, n in BEHIND:
                    if when == g:
                        post(b, n)
            for n in range(POST):
                post(1, n)

            def gather(e):
                ps = turn[e % 2]
                pe.wait_ge(xs_in[e], 32)
                if e == 0:
                    pe.wait_ge(turn_free, full[0])
                if e > 1:
                    pe.wait_ge(xsT_ready, e - 1)
                for n in range(ST):
                    m = P if n < ST - 1 else LAST
                    mm = pe.transpose(ps[:, n * P:n * P + m], xs[0:m, e, n, 0:D], identf[0:m, 0:m])
                mm.then_inc(xsT_ps, 1)

            def up(e):
                pe.wait_ge(w_split, e + 1)
                pe.wait_ge(xsT_ready, e + 1)
                if e == 0:
                    pe.wait_ge(sc_free, 3 * NG)
                for c in range(FC):
                    if e:
                        pe.wait_ge(h_ready, FC * (e - 1) + c + 1)
                    for wp, xp in PRODUCTS:
                        mm = pe.matmul(sc[:, c, 0:SLOTS], w1_part[:, e, wp, c * P:c * P + P],
                                       xsT[:, e % 2, xp, :], start=(wp == xp == 0), stop=(wp == 1))
                    mm.then_inc(h_ps, 1)

            def down(e):
                ps = (sc1, av)[e % 2]
                if e >= 2:
                    pe.wait_ge(y_ready, e - 1)
                pe.wait_ge(h_split, 2 * e + 2)
                for n in range(ST):
                    for c in range(FC):
                        for hp, wp in PRODUCTS:
                            mm = pe.matmul(ps[:, n * D:n * D + D], hT_part[:, e % 2, hp, c, n * P:n * P + P],
                                           w2_part(e)[:, wp, c, :], start=(n == 0 and c == 0 and hp == wp == 0),
                                           stop=(c == FC - 1 and hp == 1), skip_group_check=True)
                mm.then_inc(y_ps, 1)

            gather(0)
            for e in range(E):
                up(e)
                if e + 1 < E:
                    gather(e + 1)
                if e:
                    down(e - 1)
            down(E - 1)

        @block.vector
        def _(dve):
            steps, uses, banks, norms = [0], [0], [0], [0]

            def step(ins):
                steps[0] += 1
                ins.then_inc(vec_step, 1)
                dve.wait_ge(vec_step, steps[0])

            def bank():
                uses[0] += 1
                dve.wait_ge(turn_full, uses[0])
                banks[0] += 1
                return turn[(banks[0] - 1) % 2]

            def pass_bank():
                banks[0] += 1

            def layernorm(b, src, dst, ready):
                tiles = range(QT * b, QT * b + QT)
                for t in tiles:
                    last = dve.bn_stats(stats[:, t, :], src[:, t, :])
                step(last)
                for t in tiles:
                    last = dve.bn_aggr(mean_var[:, t, :], stats[:, t, :])
                step(last)
                v = mean_var[:, QT * b:QT * b + QT, 1]
                dve.tensor_scalar(v, v, EPS, None, ALU.add).then_inc(var_ready, 1)
                norms[0] += 1
                dve.wait_ge(rstd_ready, norms[0])
                for t in tiles:
                    last = dve.tensor_scalar(dst[:, t, 0:D], src[:, t, :], mean_var[:, t, 0:1],
                                             rstd[:, t:t + 1], ALU.subtract, ALU.mult)
                last.then_inc(ready, 1)

            def maxima(b, todo):
                for qt, h0, nh, keys in todo:
                    ps = bank()
                    dve.tensor_reduce(top[:, b, qt, h0:h0 + nh],
                                      ps[:, 0:nh * keys].rearrange("p (h k) -> p h k", h=nh),
                                      AX.X, ALU.max).then_inc(turn_free, 1)

            def split_maxima(g):
                b, i = divmod(g, 4)
                dve.wait_ge(turn_free, uses[0])
                heads = slice(4 * i, 4 * i + 4)
                step(dve.tensor_copy(top2[:, :, heads, 3 * HD], top[:, b, :, heads]))
                dve.tensor_tensor(top2[:, :, heads, 3 * HD + 1], top[:, b, :, heads],
                                  top2[:, :, heads, 3 * HD], ALU.subtract).then_inc(top_ready, 1)

            def low_parts(g):
                t = g % 2
                dve.wait_ge(sc_free, 3 * g + 2)
                if g >= 2:
                    dve.wait_ge(pv_done, g - 1)
                dve.tensor_tensor(p0_part[:, t, 1], p0[:, t], p0_part[:, t, 0], ALU.subtract).then_inc(p_low, 1)
                dve.wait_ge(sc_free, 3 * g + 3)
                dve.tensor_tensor(p1_part[:, t, 1], p1[:, t], p1_part[:, t, 0], ALU.subtract).then_inc(p_low, 1)

            def copy_values(g):
                dve.wait_ge(pv_done, g + 1)
                dve.tensor_copy(oT[:, g % 2, :], av[:, :]).then_inc(oT_ready, 1)

            def normalise(g):
                ps = bank()[:, 0:QT * 4 * OW].rearrange("p (t j d) -> p t j d", t=QT, j=4)
                step(dve.reciprocal(inv[:, g], ps[:, :, :, HD]))
                dve.tensor_tensor(attn[:, :, g % 4], ps[:, :, :, 0:HD],
                                  inv[:, g].unsqueeze(3).to_broadcast([P, QT, 4, HD]),
                                  ALU.mult).then_inc(turn_free, 1)

            def copy_turned(dst):
                ps = bank()
                dve.tensor_copy(dst, ps[:, 0:S]).then_inc(turn_free, 1)

            def residual(b):
                tiles = slice(QT * b, QT * b + QT)
                ps = bank()
                dve.wait_ge(gate_ready, 1)
                dve.scalar_tensor_tensor(x1[:, tiles, :].rearrange("p t d -> p (t d)"), ps[:, :], gate[:, 0:1],
                                         X[:, tiles, :].rearrange("p t d -> p (t d)"),
                                         ALU.mult, ALU.add).then_inc(turn_free, 1)
                dve.wait_ge(turn_free, uses[0])
                layernorm(b, x1, rows, rows_ready)

            def choose(b):
                ps = bank()
                dve.tensor_copy(logits[:, :, :].rearrange("p t e -> p (t e)"),
                                ps[:, 0:QT * E]).then_inc(turn_free, 1)
                dve.wait_ge(turn_free, uses[0])
                for t in range(QT):
                    last = dve.max(best[:, t, :], logits[:, t, :])
                step(last)
                for t in range(QT):
                    last = dve.max_index(best_at[:, t, :], best[:, t, :], logits[:, t, :])
                step(last)
                step(dve.tensor_copy(chosen[:, :, :], best_at[:, :, 0:TOPK]))
                dve.wait_ge(consts3, 2)
                oh = onehot[:, QT * b:QT * b + QT].rearrange("p t k e -> p (t k) e")
                dve.tensor_tensor(oh, expert_no[:, :].unsqueeze(1).to_broadcast([P, QT * TOPK, E]),
                                  chosen[:, :, :].rearrange("p t k -> p (t k)").unsqueeze(2)
                                  .to_broadcast([P, QT * TOPK, E]), ALU.is_equal).then_inc(onehot_ready, 1)
                dve.tensor_tensor(diff[:, QT * b:QT * b + QT], best[:, :, 1], best[:, :, 0],
                                  ALU.subtract).then_inc(diff_ready, 1)
                dve.wait_ge(onehot_ready, b + 1)
                oh4 = oh.rearrange("p (t k) e -> p t (k e)", k=TOPK)
                step(dve.tensor_tensor(picked[:, :, :].rearrange("p (t k) e -> p t (k e)", k=TOPK), oh4,
                                       base[:, :, :].rearrange("p k e -> p (k e)").unsqueeze(1)
                                       .to_broadcast([P, QT, TOPK * E]), ALU.mult))
                step(dve.tensor_reduce(first[:, :], picked[:, :, :], AX.X, ALU.add))

            def place(b):
                ps = bank()
                oh = onehot[:, QT * b:QT * b + QT].rearrange("p t k e -> p (t k) e")
                dve.tensor_tensor(picked[:, :, :], ps[:, 0:QT * TOPK * E].rearrange("p (c e) -> p c e", e=E),
                                  oh, ALU.mult).then_inc(turn_free, 1)
                dve.wait_ge(turn_free, uses[0])
                step(dve.tensor_reduce(rank[:, :], picked[:, :, :], AX.X, ALU.add))
                dve.tensor_scalar(over[:, :], rank[:, :], float(CAP), FAR, ALU.is_gt, ALU.mult)
                step(dve.tensor_tensor(first[:, :], first[:, :], rank[:, :], ALU.add))
                dve.tensor_tensor(slot_of[:, QT * TOPK * b:QT * TOPK * (b + 1)], first[:, :], over[:, :],
                                  ALU.add).then_inc(slot_ready, 1)

            dve.memset(pack_raw[:, :, :, :, :, :, :], 0.0).then_inc(cleared, 1)
            dve.memset(v0[:, :, :, :], 0.0)
            dve.memset(v1[:, :, :, :, :], 0.0).then_inc(cleared, 1)
            dve.memset(top2[:, :, :, :], 0.0).then_inc(cleared, 1)
            for b in range(B):
                dve.wait_ge(x_in[b], 16)
                layernorm(b, X, xn, xn_ready)
            dve.wait_ge(kT_ready, 1)
            step(dve.tensor_copy(kT_part[:, 0], kT[:, :, :]))
            dve.tensor_tensor(kT_part[:, 1], kT[:, :, :], kT_part[:, 0], ALU.subtract).then_inc(kT_split, 1)
            dve.tensor_tensor(kTr[:, 0, 0:FIRST_HEADS],
                              kT_part[:, 0, 0, 0:C].unsqueeze(1).to_broadcast([P, FIRST_HEADS, C]),
                              head_mask[:, :, :].rearrange("p i j -> p (i j)")[:, 0:FIRST_HEADS].unsqueeze(2)
                              .to_broadcast([P, FIRST_HEADS, C]), ALU.mult).then_inc(kTr_first, 1)
            dve.wait_ge(consts2, 1)
            dve.tensor_reduce(minus_one[:, :], minus_raw[:, :, :], AX.XY, ALU.add).then_inc(minus_ready, 1)
            for b in range(B):
                dve.wait_ge(q_high, b + 1)
                dve.tensor_tensor(qT[:, 1, b, :], sc[:, 2 + b, :], qT[:, 0, b, :],
                                  ALU.subtract).then_inc(q_ready, 1)
            dve.wait_ge(cleared, 3)
            maxima(0, maxima_todo[0])
            split_maxima(0)
            pass_bank()

            def after(b, n):
                if n == 0:
                    copy_turned(attnT[:, :])
                if n == 1:
                    residual(b)
                if n == 2:
                    copy_turned(rowsT[:, :])
                if n == 3:
                    choose(b)
                if n == 4:
                    place(b)

            for g in range(NG + 2):
                for n in groups_ahead(g):
                    maxima(n // 4, maxima_todo[n % 4])
                    split_maxima(n)
                    if n != g + 2:
                        pass_bank()
                for when, b, n in BESIDE:
                    if when == g:
                        after(b, n)
                if 1 <= g <= NG:
                    copy_values(g - 1)
                if g + 2 < NG:
                    pass_bank()
                if g >= 2:
                    normalise(g - 2)
                if g < NG:
                    low_parts(g)
                for when, b, n in BEHIND:
                    if when == g:
                        after(b, n)
            for n in range(POST):
                after(1, n)

            dve.wait_ge(ediff_ready, B)
            step(dve.tensor_scalar(weight[:, :, 1], ediff[:, :], 1.0, None, ALU.add))
            step(dve.reciprocal(diff[:, :], weight[:, :, 1]))
            step(dve.tensor_scalar(weight[:, :, 0], diff[:, :], gate[:, 1:2], None, ALU.mult))
            step(dve.tensor_tensor(weight[:, :, 1], weight[:, :, 0], ediff[:, :], ALU.mult))

            def slots_turned(e):
                dve.wait_ge(xsT_ps, e + 1)
                if e >= 2:
                    dve.wait_ge(h_ps, FC * (e - 1))
                ps = turn[e % 2][:, 0:SLOTS]
                step(dve.tensor_copy(xsT[:, e % 2, 0, :], ps))
                dve.tensor_tensor(xsT[:, e % 2, 1, :], ps, xsT[:, e % 2, 0, :], ALU.subtract).then_inc(xsT_ready, 1)
                dve.tensor_tensor(result_of[:, e, 0:ST - 1], xs[:, e, 0:ST - 1, D], choice_row[:, 0:ST - 1],
                                  ALU.add)
                dve.tensor_tensor(result_of[0:LAST, e, ST - 1:ST], xs[0:LAST, e, ST - 1, D:D + 1],
                                  choice_row[0:LAST, ST - 1:ST], ALU.add)

            def results_out(e):
                ps = (sc1, av)[e % 2]
                dve.wait_ge(y_ps, e + 1)
                if e >= 2:
                    dve.wait_ge(back, 16 * ST * (e - 1))
                full = (ST - 1) * D
                dve.tensor_tensor(y[:, e % 2, 0:ST - 1, :], ps[:, 0:full].rearrange("p (n d) -> p n d", d=D),
                                  B2[:, e, :].unsqueeze(1).to_broadcast([P, ST - 1, D]), ALU.add)
                dve.tensor_tensor(y[0:LAST, e % 2, ST - 1, :], ps[0:LAST, full:full + D], B2[0:LAST, e, :],
                                  ALU.add).then_inc(y_ready, 1)

            def split_hidden(e):
                t = e % 2
                if e >= 2:
                    dve.wait_ge(y_ps, e - 1)
                for c in range(0, FC, 2):
                    dve.wait_ge(h_ready, FC * e + c + 2)
                    h = hT[:, t, c:c + 2, :]
                    step(dve.tensor_copy(hT_part[:, t, 0, c:c + 2, 0:SLOTS], h))
                    dve.tensor_tensor(hT_part[:, t, 1, c:c + 2, 0:SLOTS], h, hT_part[:, t, 0, c:c + 2, 0:SLOTS],
                                      ALU.subtract).then_inc(h_split, 1)

            dve.wait_ge(wo_in, 32)
            dve.memset(hT_part[:, :, :, :, SLOTS:ST * P].bitcast(F32), 0.0)
            slots_turned(0)
            for e in range(E):
                if e + 1 < E:
                    slots_turned(e + 1)
                split_hidden(e)
                if e >= 1:
                    results_out(e - 1)
            results_out(E - 1)

            n = NT // NPIECES
            for c in range(NPIECES):
                dve.wait_ge(yk_in[c], 32)
                for k in range(TOPK):
                    for t in range(n * c, n * c + n):
                        last = dve.scalar_tensor_tensor(fin[:, t, :], yk[:, k, t, :], weight[:, t, k:k + 1],
                                                        (fin if k else x1)[:, t, :], ALU.mult, ALU.add)
                        if k:
                            last.then_inc(fin_ready, 1)
                    if not k:
                        step(last)


def kernel(x, ctx_1024, g_xattn, g_ffn, L0_xattn_Wq, L0_xattn_Wk, L0_xattn_Wv, L0_xattn_Wo,
           L0_ffn_Wr, L0_ffn_W1, L0_ffn_b1, L0_ffn_W2, L0_ffn_b2):
    import numpy as np
    from concourse import bacc
    from concourse.bass_utils import run_bass_kernel_spmd

    woT = np.transpose(np.reshape(L0_xattn_Wo, (D, 4, 4, HD)), (2, 1, 3, 0)).reshape(D, D)
    arrays = {
        "x": np.reshape(x, (T, D)),
        "ctxT": np.transpose(ctx_1024, (2, 0, 1)),
        "gx": g_xattn,
        "gf": g_ffn,
        "wqT": np.transpose(L0_xattn_Wq),
        "wkT": np.transpose(L0_xattn_Wk),
        "wvT": np.transpose(L0_xattn_Wv),
        "woT": woT,
        "wr": L0_ffn_Wr,
        "w1": L0_ffn_W1,
        "b1T": np.transpose(np.reshape(L0_ffn_b1, (E, FC, P)), (2, 0, 1)),
        "w2": L0_ffn_W2,
        "b2": L0_ffn_b2,
    }
    nc = bacc.Bacc("TRN2", target_bir_lowering=False, num_devices=1)
    args = []
    for name, a in arrays.items():
        arrays[name] = a = np.ascontiguousarray(a)
        args.append(nc.dram_tensor(name, a.shape, mybir.dt.from_np(a.dtype), kind="ExternalInput").ap())
    out = nc.dram_tensor("out", (T, D), F32, kind="ExternalOutput").ap()
    build(nc, *args, out)
    done = run_bass_kernel_spmd(nc, [arrays], core_ids=[0])
    return done.results[0]["out"].reshape(B, S, D)
```

```python
from contextlib import ExitStack

import concourse.bass as bass
from concourse import mybir

F32 = mybir.dt.float32
F32R = mybir.dt.float32r
BF16 = mybir.dt.bfloat16
F16 = mybir.dt.float16
U32 = mybir.dt.uint32
ALU = mybir.AluOpType
ACT = mybir.ActivationFunctionType
AX = mybir.AxisListType

P = 128
B, S, D = 2, 512, 128
C = 154
H, HD = 16, 8
T = B * S
NT = T // P
QT = S // P
C1 = C - P
CP = P + 32
Q1 = S - P
E, F = 8, 512
FC = F // P
TOPK = 2
CAP = max(1, int(T * 1.25 / E))
SLOTS = TOPK * CAP
ST = -(-SLOTS // P)
LAST = SLOTS - (ST - 1) * P
ROW = 132
SCALE = float(HD) ** -0.5
NEG = -1e30
EPS = 1e-5
FAR = 8192.0
OW = HD + 1
NG = 4 * B
VW = 32
SPLIT_FIRST = 4
PRODUCTS = ((0, 0), (0, 1), (1, 0))
PARTS = 3


def groups_of_heads(qt):
    if qt == 0:
        return [(4 * n, 4, P) for n in range(4)]
    return [(0, 3, C), (3, 3, C), (6, 3, C), (9, 3, C), (12, 2, C), (14, 2, C)]


def build(nc, x, ctxT, gx, gf, wqT, wkT, wvT, woT, wr, w1, b1T, w2, b2T, out):
    with ExitStack() as stack:
        def sb(name, shape, dt=F32):
            return stack.enter_context(nc.sbuf_tensor(name, shape, dt))

        def psum(name, shape, dt=F32):
            return stack.enter_context(nc.psum_tensor(name, shape, dt))

        def sem(name):
            return stack.enter_context(nc.semaphore(name))

        slots = nc.dram_tensor("slots", (E * SLOTS, ROW), F32, kind="Internal").ap()
        results = nc.dram_tensor("results", (TOPK * T, D), F32, kind="Internal").ap()

        X = sb("X", [P, NT, D])
        CT = sb("CT", [P, B, P + 4 * 32])
        WQ, WK, WV, WO = (sb(n, [P, D]) for n in ("WQ", "WK", "WV", "WO"))
        WR = sb("WR", [P, E])
        W1 = sb("W1", [P, 2, F])
        B1 = sb("B1", [P, E, FC])
        W2 = sb("W2", [P, 2, FC, D])
        B2 = sb("B2", [P, E])
        G = sb("G", [P, 2])
        zeros = sb("zeros", [P, D])
        slot0 = sb("slot0", [P, ROW])
        identf = sb("identf", [P, P])
        identb = sb("identb", [P, P], BF16)
        head_mask = sb("head_mask", [P, 4, 4])
        block_mask = sb("block_mask", [P, 4])
        minus_raw = sb("minus_raw", [P, 4, 2])
        minus_one = sb("minus_one", [P, 1])
        pack_q = sb("pack_q", [P, 2, 4, 4, 4, HD], F32R)
        mask_q = sb("mask_q", [P, 4, P], BF16)
        mask_k0 = sb("mask_k0", [P, P], BF16)
        mask_k1 = sb("mask_k1", [P, 32], BF16)
        fold = sb("fold", [P, 4, OW])
        upto = sb("upto", [P, P], BF16)
        ones = sb("ones", [P, P], BF16)
        expert_no = sb("expert_no", [P, E])
        base = sb("base", [P, TOPK, E])
        choice_row = sb("choice_row", [P, ST])
        half = sb("half", [P, NT])
        stats = sb("stats", [P, NT, 6])
        mean_var = sb("mean_var", [P, NT, 2])
        rstd = sb("rstd", [P, NT])
        xn_all = sb("xn_all", [P, 2 * NT * D])
        xn = xn_all[:, 0:NT * D].rearrange("p (n d) -> p n d", n=NT)
        xnT = xn_all[:, NT * D:2 * NT * D].rearrange("p (b q) -> p b q", b=B)
        q_all = sb("q_all", [P, 2 * B * S], F32R)
        qT = q_all[:, :].rearrange("p (w b q) -> p w b q", w=2, b=B)
        kT = sb("kT", [P, B, CP])
        kT_part = sb("kT_part", [P, 2, B, CP], F32R)
        shared = sb("shared", [P, B * H * C + B * 4 * P], F32R)
        kTr = shared[:, 0:B * H * C].rearrange("p (b h k) -> p b h k", b=B, h=H)
        q_pack_all = sb("q_pack_all", [P, 4 * B * S], F32R)
        q_pack = q_pack_all[:, :].rearrange("p (i b q) -> p i b q", i=4, b=B)
        pack_k = q_pack_all[:, 0:2 * 4 * P].rearrange("p (w i j s d) -> p w i j s d", w=2, i=4, j=4, s=4)
        w1_all = sb("w1_all", [P, E * 2 * F], F32R)
        k_pack = w1_all[:, SPLIT_FIRST * 2 * F:SPLIT_FIRST * 2 * F + 4 * B * CP].rearrange(
            "p (i b k) -> p i b k", i=4, b=B)
        k1 = shared[:, B * H * C:B * H * C + B * 4 * P].rearrange("p (b i j k) -> p b i j k", b=B, i=4, j=4)
        vs = sb("vs", [P, 2 * B, H, PARTS, HD], BF16)
        v0 = sb("v0", [P, B, H, VW], BF16)
        v1 = sb("v1", [P, B, 4, 4, VW], BF16)
        top = sb("top", [P, B, QT, H])
        top2 = sb("top2", [P, QT, H, 4 * HD], BF16)
        p0_all = sb("p0_all", [P, 2 * 4 * S])
        p0 = p0_all[:, :].rearrange("p (t j q) -> p t j q", t=2, j=4)
        p1 = sb("p1", [P, 2, Q1])
        parts_all = sb("parts_all", [P, 2 * 2 * 4 * S], F16)
        p0_part = parts_all[:, :].rearrange("p (t w j q) -> p t w j q", t=2, w=2, j=4)
        pack_raw = parts_all[:, 0:2 * 2 * 2 * 4 * P].bitcast(F32).rearrange(
            "p (k w i j s d) -> p k w i j s d", k=2, w=2, i=4, j=4, s=4)
        w_late = p0_all[:, :].rearrange("p (e w f) -> p e w f", e=E - SPLIT_FIRST, w=2)
        p1_part = sb("p1_part", [P, 2, 2, Q1], F16)
        oT = sb("oT", [P, 2, S])
        v_rest = oT[:, :, :].rearrange("p w (b d) -> p w b d", b=2 * B)
        inv = sb("inv", [P, NG, QT, 4])
        attn = sb("attn", [P, QT, 4, 4, HD])
        attnT = CT[:, :, :].rearrange("p b k -> p (b k)")
        gate = sb("gate", [P, 2])
        x1 = X
        rows = sb("rows", [P, NT, ROW])
        rowsT = sb("rowsT", [P, S])
        logits = sb("logits", [P, NT, E])
        best = sb("best", [P, NT, E])
        best_at = sb("best_at", [P, NT, E], U32)
        chosen = sb("chosen", [P, NT, TOPK])
        onehot = sb("onehot", [P, NT, TOPK, E], BF16)
        diff = sb("diff", [P, NT])
        ediff = sb("ediff", [P, NT])
        weight = sb("weight", [P, NT, TOPK])
        picked = sb("picked", [P, NT * TOPK, E])
        rank = sb("rank", [P, NT * TOPK])
        first = sb("first", [P, NT * TOPK])
        over = sb("over", [P, NT * TOPK])
        slot_of = sb("slot_of", [P, NT * TOPK], U32)
        xs = parts_all[:, 0:2 * E * ST * ROW].bitcast(F32).rearrange("p (e n r) -> p e n r", e=E, n=ST)
        xsT = q_all[:, 0:2 * 2 * SLOTS].rearrange("p (t w s) -> p t w s", t=2, w=2)
        hT = p0_all[:, 0:2 * FC * SLOTS].rearrange("p (t c s) -> p t c s", t=2, c=FC)
        hT_part = shared[:, 0:2 * 2 * FC * SLOTS].rearrange("p (t w c s) -> p t w c s", t=2, w=2, c=FC)
        w1_part = w1_all[:, :].rearrange("p (e w f) -> p e w f", e=E, w=2)
        w2_low = sb("w2_low", [P, SPLIT_FIRST, 2, FC, D], F32R)
        w2_high = q_pack_all[:, 0:(E - SPLIT_FIRST) * 2 * FC * D].rearrange(
            "p (e w c d) -> p e w c d", e=E - SPLIT_FIRST, w=2, c=FC)

        def w1_whole(e):
            return W1[:, e % 2] if e < SPLIT_FIRST else w_late[:, e - SPLIT_FIRST, 0]

        def w2_whole(e):
            return W2[:, e % 2] if e < SPLIT_FIRST else w_late[:, e - SPLIT_FIRST, 1].rearrange(
                "p (c d) -> p c d", c=FC)

        def w2_part(e):
            return w2_low[:, e] if e < SPLIT_FIRST else w2_high[:, e - SPLIT_FIRST]

        y = p1[:, :, :].rearrange("p t (n d) -> p t n d", d=D)
        gelu_first = sb("gelu_first", [P, 1])
        yT = sb("yT", [P, 2, ST * P])
        result_of = sb("result_of", [P, E, ST], U32)
        yk = xn_all[:, :].rearrange("p (n k d) -> p n k d", k=TOPK, n=NT)
        fin = X

        sc = psum("sc", [P, 4, 512])
        sc1 = psum("sc1", [P, 512])
        av = psum("av", [P, 512])
        turn = [psum(f"turn{n}", [P, 512]) for n in range(2)]

        x_in = [sem(f"x_in{b}") for b in range(B)]
        ctx_in, ctx_rep, wk_in, wv_in, wq_in, wo_in, small_in = (
            sem(n) for n in ("ctx_in", "ctx_rep", "wk_in", "wv_in", "wq_in", "wo_in", "small_in"))
        w_in = [sem(f"w_in{e}") for e in range(E)]
        pool_step = sem("pool_step")
        zero_ready = sem("zero_ready")
        consts1, consts2, consts3 = sem("consts1"), sem("consts2"), sem("consts3")
        laid = sem("laid")
        vec_step = sem("vec_step")
        var_ready, rstd_ready, xn_ready = sem("var_ready"), sem("rstd_ready"), sem("xn_ready")
        kv_ps, kT_ready, v_copied, v_ready = (sem(n) for n in ("kv_ps", "kT_ready", "v_copied", "v_ready"))
        minus_ready, k_packed_ps, k_packed = sem("minus_ready"), sem("k_packed_ps"), sem("k_packed")
        q_packed_ps, q_packed = sem("q_packed_ps"), sem("q_packed")
        kT_split, kTr_first, kTr_ready, k_ready = sem("kT_split"), sem("kTr_first"), sem("kTr_ready"), sem("k_ready")
        xnT_ps, xnT_ready, q_ps, q_high, q_ready = (
            sem(n) for n in ("xnT_ps", "xnT_ready", "q_ps", "q_high", "q_ready"))
        turn_full, turn_free = sem("turn_full"), sem("turn_free")
        top_ready, pack_raw_ready, pack_ready = sem("top_ready"), sem("pack_raw_ready"), sem("pack_ready")
        sc_full, sc_free, pv_done = sem("sc_full"), sem("sc_free"), sem("pv_done")
        p_low, p1_low = sem("p_low"), sem("p1_low")
        oT_ready = sem("oT_ready")
        w_high, w_split, w_late_split = sem("w_high"), sem("w_split"), sem("w_late_split")
        fold_made = sem("fold_made")
        cleared, v_part, v_left = sem("cleared"), sem("v_part"), sem("v_left")
        gate_ready = sem("gate_ready")
        rows_ready = sem("rows_ready")
        onehot_ready, slot_ready = sem("onehot_ready"), sem("slot_ready")
        diff_ready, ediff_ready = sem("diff_ready"), sem("ediff_ready")
        sent = sem("sent")
        xs_in = [sem(f"xs_in{e}") for e in range(E)]
        xsT_high = sem("xsT_high")
        xsT_ps, xsT_ready = sem("xsT_ps"), sem("xsT_ready")
        h_ps, h_ready, h_split = sem("h_ps"), sem("h_ready"), sem("h_split")
        yT_ps, yT_ready, y_ps, y_ready = sem("yT_ps"), sem("yT_ready"), sem("y_ps"), sem("y_ready")
        back = [sem(f"back{n}") for n in range(2)]
        padded, result_rows = sem("padded"), sem("result_rows")
        yk_in = [sem(f"yk_in{n}") for n in range(4)]
        weights_ready, second_ready = sem("weights_ready"), sem("second_ready")
        fin_ready, stored = sem("fin_ready"), sem("stored")

        x_d = x.rearrange("(n p) d -> p n d", p=P)
        out_d = out.rearrange("(n p) d -> p n d", p=P)
        res_d = results.rearrange("(n p k) d -> p n (k d)", p=P, k=TOPK)

        blocks = ((0, QT), (QT, QT + 2), (QT + 2, NT))
        LATER = [(1, 0), (2, 0), (1, 1), (2, 1), (1, 2), (2, 2), (1, 3), (1, 4), (2, 3), (2, 4)]
        NPIECES = 4
        BESIDE = [(6, 0, 1), (7, 0, 2)]
        BEHIND = [(5, 0, 0), (7, 0, 3), (8, 0, 4)]
        maxima_todo = [(b, qt, *h) for b in range(B) for i in range(4) for qt in range(QT)
                       for h in groups_of_heads(qt) if h[0] // 4 == i]
        shares = (7, 4, 6, 6, 6, 5, 5, 5)
        maxima_first = maxima_todo[:shares[0]]
        FIRST_HEADS = 6

        def maxima_beside(g, n):
            todo = maxima_todo[sum(shares[:g + 1]):sum(shares[:g + 2])]
            cut = (0, 1, 2, 3, None)
            return todo[cut[n]:cut[n + 1]]

        turns = shares[0] * ["maximum"] + [("pack", 0)]
        for g in range(NG + 2):
            turns += ["maximum" for n in range(3) for _ in maxima_beside(g, n)]
            turns += [("fold", g - 2)] if g >= 2 else []
            turns += ["maximum" for _ in maxima_beside(g, 3)]
            turns += ["after" for when, _, _ in BESIDE if when == g]
            turns += [("pack", g + 1)] if g + 1 < NG else []
            turns += ["after" for when, _, _ in BEHIND if when == g]

        def fold_use(g):
            return sum(t[0] != "pack" for t in turns[:turns.index(("fold", g)) + 1])

        block = stack.enter_context(nc.Block())

        @block.sync
        def _(sp):
            sp.dma_start(X[:, 0:QT, :], x_d[:, 0:QT, :]).then_inc(x_in[0], 16)
            sp.dma_start(CT[:, :, 0:C], ctxT[:, :, 0:C]).then_inc(ctx_in, 16)
            sp.dma_start(CT[:, :, C:CP], ctxT[:, :, 0:CP - C]).then_inc(ctx_in, 16)
            sp.dma_start(X[:, QT:NT, :], x_d[:, QT:NT, :]).then_inc(x_in[1], 16)
            sp.dma_start(WV[:, :], wvT).then_inc(wv_in, 16)
            sp.wait_ge(zero_ready, 1)
            sp.dma_start(slots.rearrange("(p n) r -> p n r", p=P),
                         slot0[:, :].unsqueeze(1).to_broadcast([P, E * SLOTS // P, ROW])).then_inc(laid, 16)
            sp.dma_start(results.rearrange("(p n) d -> p n d", p=P),
                         zeros[:, :].unsqueeze(1).to_broadcast([P, TOPK * T // P, D])).then_inc(laid, 16)
            sp.dma_start(G[:, 0:1], gx.partition_broadcast(P)).then_inc(small_in, 16)
            sp.dma_start(G[:, 1:2], gf.partition_broadcast(P)).then_inc(small_in, 16)
            sp.dma_start(WR[:, :], wr).then_inc(small_in, 16)
            sp.dma_start(B1[:, :, :], b1T).then_inc(small_in, 16)
            sp.dma_start(WO[:, :], woT).then_inc(wo_in, 16)
            sp.dma_start(B2[:, :], b2T).then_inc(wo_in, 16)
            for e in range(E):
                if 2 <= e < SPLIT_FIRST:
                    sp.wait_ge(w_split, e - 1)
                if e == SPLIT_FIRST:
                    sp.wait_ge(p_low, 2 * NG)
                sp.dma_start(w1_whole(e), w1[e]).then_inc(w_in[e], 16)
                sp.dma_start(w2_whole(e), w2[e].rearrange("(c p) d -> p c d", p=P)).then_inc(w_in[e], 16)
            sp.wait_ge(sent, 16 * NT * TOPK)
            for e in range(E):
                full = slots[e * SLOTS:e * SLOTS + (ST - 1) * P, :].rearrange("(n p) r -> p n r", p=P)
                sp.dma_start(xs[:, e, 0:ST - 1, :], full).then_inc(xs_in[e], 16)
                sp.dma_start(xs[0:LAST, e, ST - 1, :],
                             slots[e * SLOTS + (ST - 1) * P:(e + 1) * SLOTS, :]).then_inc(xs_in[e], 16)
            for n in range(2):
                sp.wait_ge(back[n], 16 * E // 2 * ST)
            n = NT // NPIECES
            for c in range(NPIECES):
                sp.dma_start(yk[:, n * c:n * c + n].rearrange("p n k d -> p n (k d)"),
                             res_d[:, n * c:n * c + n, :]).then_inc(yk_in[c], 16)
            for c in range(NPIECES):
                sp.wait_ge(fin_ready, c + 1)
                sp.dma_start(out_d[:, n * c:n * c + n, :], fin[:, n * c:n * c + n, :]).then_inc(stored, 16)
            sp.wait_ge(stored, 16 * NPIECES)

        @block.gpsimd
        def _(pool):
            steps = [0]

            def step(ins):
                steps[0] += 1
                ins.then_inc(pool_step, 1)
                pool.wait_ge(pool_step, steps[0])

            pool.memset(zeros[:, :], 0.0)
            step(pool.memset(slot0[:, :], 0.0))
            step(pool.memset(slot0[:, D:D + 1], FAR))
            pool.memset(half[:, :], -0.5).then_inc(zero_ready, 1)
            pool.memset(identf[:, :], 0.0)
            step(pool.memset(head_mask[:, :, :], 1.0))
            step(pool.affine_select(out=identf[:, :], in_=identf[:, :], compare_op=ALU.not_equal, fill=1.0,
                                    base=0, pattern=[[-1, P]], channel_multiplier=1))
            step(pool.affine_select(out=head_mask[:, :, :], in_=head_mask[:, :, :], compare_op=ALU.is_ge,
                                    fill=0.0, base=0, pattern=[[-HD, 4], [-32, 4]], channel_multiplier=1))
            pool.affine_select(out=head_mask[:, :, :], in_=head_mask[:, :, :], compare_op=ALU.is_ge,
                               fill=0.0, base=HD - 1, pattern=[[HD, 4], [32, 4]],
                               channel_multiplier=-1).then_inc(consts1, 1)
            step(pool.memset(minus_raw[:, :, :], 0.0))
            step(pool.affine_select(out=minus_raw[:, :, :], in_=minus_raw[:, :, :], compare_op=ALU.not_equal,
                                    fill=-1.0, base=-3 * HD, pattern=[[-32, 4], [-1, 2]],
                                    channel_multiplier=1))

            def packing(dst, part_of):
                for pair, part in enumerate(part_of):
                    m = dst[:, part, :, :, pair, :]
                    last = pool.affine_select(out=m, in_=m, compare_op=ALU.not_equal, fill=1.0, base=0,
                                              pattern=[[-HD, 4], [-32, 4], [-1, HD]], channel_multiplier=1)
                return last

            def root(tiles, n):
                pool.wait_ge(var_ready, n)
                nc.gpsimd.tensor_tensor(rstd[:, slice(*tiles)], mean_var[:, slice(*tiles), 1],
                                        half[:, slice(*tiles)], ALU.pow).then_inc(rstd_ready, 1)

            step(pool.memset(mask_q[:, :, :], 0.0))
            pool.affine_select(out=mask_q[:, :, :], in_=mask_q[:, :, :], compare_op=ALU.is_ge, fill=NEG,
                               base=0, pattern=[[0, 4], [-1, P]], channel_multiplier=1)
            pool.tensor_copy(identb[:, :], identf[:, :]).then_inc(consts2, 1)
            root((0, QT), 1)
            pool.wait_ge(ctx_in, 32)
            for b in range(B):
                pool.tensor_copy(CT[:, b, CP:P + 4 * 32].rearrange("p (j k) -> p j k", k=32),
                                 CT[:, b, P:CP].unsqueeze(1).to_broadcast([P, 3, 32])).then_inc(ctx_rep, 1)
            pool.wait_ge(cleared, 1)
            packing(pack_raw[:, 0], [kp for kp, qp in PRODUCTS]).then_inc(pack_raw_ready, 1)
            packing(pack_raw[:, 1], [qp for kp, qp in PRODUCTS]).then_inc(pack_raw_ready, 1)
            root((QT, NT), 2)
            pool.wait_ge(cleared, 2)
            step(pool.memset(v0[:, :, :, PARTS * HD:PARTS * HD + 1], 1.0))
            for j in range(4):
                step(pool.memset(v1[32 * j:32 * j + C1, :, :, j, PARTS * HD:PARTS * HD + 1], 1.0))
            step(pool.memset(block_mask[:, :], 1.0))
            step(pool.affine_select(out=block_mask[:, :], in_=block_mask[:, :], compare_op=ALU.is_ge,
                                    fill=0.0, base=0, pattern=[[-32, 4]], channel_multiplier=1))
            step(pool.affine_select(out=block_mask[:, :], in_=block_mask[:, :], compare_op=ALU.is_ge,
                                    fill=0.0, base=31, pattern=[[32, 4]], channel_multiplier=-1))

            def keys_for_max(b, h0):
                pool.tensor_tensor(kTr[:, b, h0:H],
                                   kT_part[:, 0, b, 0:C].unsqueeze(1).to_broadcast([P, H - h0, C]),
                                   head_mask[:, :, :].rearrange("p i j -> p (i j)")[:, h0:H].unsqueeze(2)
                                   .to_broadcast([P, H - h0, C]), ALU.mult).then_inc(kTr_ready, 1)

            pool.wait_ge(kT_split, 1)
            keys_for_max(0, FIRST_HEADS)
            pool.memset(mask_k1[:, :], 0.0)
            step(pool.memset(mask_k0[:, :], 0.0))
            pool.affine_select(out=mask_k0[:, :], in_=mask_k0[:, :], compare_op=ALU.is_ge, fill=NEG,
                               base=0, pattern=[[1, P]], channel_multiplier=-1)
            for j in range(4):
                m = mask_k1[32 * j:32 * j + 32, :]
                step(pool.affine_select(out=m, in_=m, compare_op=ALU.is_ge, fill=NEG, base=0,
                                        pattern=[[1, 32]], channel_multiplier=-1))
            pool.memset(ones[:, :], 1.0).then_inc(consts3, 1)
            pool.wait_ge(k_packed, 4)
            for b in range(B):
                pool.wait_ge(v_part, b + 1)
                pool.tensor_tensor(v_rest[:, b].rearrange("p b (h d) -> p b h d", h=H),
                                   v_rest[:, 1 - b].rearrange("p b (h d) -> p b h d", h=H),
                                   vs[:, :, :, b, :], ALU.subtract).then_inc(v_left, 1)
                pool.tensor_tensor(k1[:, b], k_pack[:, :, b, P:CP].unsqueeze(2).to_broadcast([P, 4, 4, 32]),
                                   block_mask[:, :].unsqueeze(1).unsqueeze(3).to_broadcast([P, 4, 4, 32]),
                                   ALU.mult).then_inc(k_ready, 1)
            step(pool.memset(fold[:, :, :], 0.0))
            for part in range(PARTS + 1):
                cols = fold[:, :, 0:HD] if part < PARTS else fold[:, :, HD:OW]
                step(pool.affine_select(out=cols, in_=cols, compare_op=ALU.not_equal, fill=1.0,
                                        base=-HD * part, pattern=[[-32, 4], [-1, HD if part < PARTS else 1]],
                                        channel_multiplier=1))
            pool.memset(upto[:, :], 1.0).then_inc(fold_made, 1)
            keys_for_max(1, 0)
            pool.wait_ge(fold_made, 1)
            pool.affine_select(out=upto[:, :], in_=upto[:, :], compare_op=ALU.is_ge, fill=0.0,
                               base=0, pattern=[[1, P]], channel_multiplier=-1)
            pool.iota(expert_no[:, :], pattern=[[1, E]], base=0, channel_multiplier=0,
                      allow_small_or_imprecise_dtypes=True)
            pool.iota(base[:, :, :], pattern=[[CAP, TOPK], [SLOTS, E]], base=-1, channel_multiplier=0,
                      allow_small_or_imprecise_dtypes=True)
            pool.memset(rows[:, :, D:ROW], 0.0)
            pool.memset(choice_row[:, 0:1], 0.0)
            step(pool.memset(choice_row[:, 1:ST], 1.0))
            step(pool.memset(choice_row[0:CAP - P, 1:2], 0.0))
            pool.iota(rows[:, :, D], pattern=[[TOPK * P, NT]], base=0, channel_multiplier=TOPK,
                      allow_small_or_imprecise_dtypes=True).then_inc(consts3, 1)

            def split_weights(n):
                e = n // 2
                pool.wait_ge(w_in[e], 32)
                w, part = ((w1_whole(e), w1_part[:, e]), (w2_whole(e), w2_part(e)))[n % 2]
                step(pool.tensor_copy(part[:, 0], w))
                last = pool.tensor_tensor(part[:, 1], w, part[:, 0], ALU.subtract)
                if n % 2:
                    last.then_inc(w_split, 1)

            splits = [0]
            for g in range(NG):
                if g == 6:
                    root(blocks[0], 3)
                t = g % 2
                pool.wait_ge(sc_free, 3 * g + 3)
                if g >= 2:
                    pool.wait_ge(pv_done, g - 1)
                pool.tensor_tensor(p1_part[:, t, 1], p1[:, t], p1_part[:, t, 0], ALU.subtract).then_inc(p1_low, 1)
                while splits[0] < min(3 * (g + 1) // 2 + (g > 0), 2 * SPLIT_FIRST):
                    split_weights(splits[0])
                    splits[0] += 1
            pool.wait_ge(laid, 32)
            pool.wait_ge(consts3, 2)
            for k, (t0, t1) in enumerate(blocks):
                pool.wait_ge(slot_ready, k + 1)
                for c in range(TOPK * t0, TOPK * t1):
                    if c == TOPK * QT - 3:
                        root(blocks[1], 4)
                        root(blocks[2], 5)
                    nc.gpsimd.indirect_dma_start(
                        out=slots, out_offset=bass.IndirectOffsetOnAxis(ap=slot_of[:, c:c + 1], axis=0),
                        in_=rows[:, c // TOPK, :], in_offset=None,
                        bounds_check=E * SLOTS - 1, oob_is_err=False).then_inc(sent, 16)
            pool.wait_ge(result_rows, 2)
            for e in range(E):
                pool.wait_ge(y_ready, e + 1)
                for n in range(ST):
                    m = P if n < ST - 1 else LAST
                    nc.gpsimd.indirect_dma_start(
                        out=results, out_offset=bass.IndirectOffsetOnAxis(ap=result_of[0:m, e, n:n + 1], axis=0),
                        in_=y[0:m, e % 2, n, :], in_offset=None,
                        bounds_check=TOPK * T - 1, oob_is_err=False).then_inc(back[e % 2], 16)

        @block.scalar
        def _(act):
            act.dma_start(WK[:, :], wkT).then_inc(wk_in, 16)
            act.dma_start(WQ[:, :], wqT).then_inc(wq_in, 16)
            act.wait_ge(kv_ps, 1)
            act.activation(kT[:, :, :], sc1[:, 0:B * CP], ACT.Copy).then_inc(kT_ready, 1)

            def turned_rows(b):
                act.wait_ge(xnT_ps, b + 1)
                act.activation(xnT[:, b, :], sc[:, b, :], ACT.Copy).then_inc(xnT_ready, 1)

            def high_queries(b):
                act.wait_ge(q_ps, b + 1)
                act.activation(qT[:, 0, b, :], sc[:, 2 + b, :], ACT.Copy).then_inc(q_high, 1)

            def packing(n):
                act.wait_ge(pack_raw_ready, n + 1)
                act.activation((pack_k, pack_q)[n][:, :, :, :, :, :], pack_raw[:, n], ACT.Copy).then_inc(pack_ready, 1)

            turned_rows(0)
            packing(0)
            high_queries(0)
            act.wait_ge(minus_ready, 1)
            for i in range(4):
                act.wait_ge(k_packed_ps, i + 1)
                act.activation(k_pack[:, i], (sc1, av)[i % 2][:, 0:B * CP].rearrange("p (b k) -> p b k", b=B),
                               ACT.Identity, bias=minus_one[:, :]).then_inc(k_packed, 1)

            def split_values(part):
                if part:
                    act.wait_ge(v_left, part)
                else:
                    act.wait_ge(v_copied, 1)
                act.activation(vs[:, :, :, part, :],
                               v_rest[:, (part + 1) % 2].rearrange("p b (h d) -> p b h d", h=H),
                               ACT.Copy).then_inc(v_part, 1)

            turned_rows(1)
            packing(1)
            act.wait_ge(kv_ps, 2)
            act.activation(v_rest[:, 1].rearrange("p b d -> p (b d)"), av[:, :],
                           ACT.Copy).then_inc(v_copied, 1)
            split_values(0)
            high_queries(1)

            def pack(g):
                act.wait_ge(q_packed_ps, g + 1)
                act.activation(q_pack[:, g % 4, g // 4, :], turn[turns.index(("pack", g)) % 2][:, :],
                               ACT.Copy).then_inc(q_packed, 1)

            act.wait_ge(k_packed, 4)
            pack(0)
            split_values(1)
            act.wait_ge(small_in, 64)
            act.activation(gate[:, :], G[:, :], ACT.Tanh).then_inc(gate_ready, 1)

            def high_weights(e):
                act.wait_ge(w_in[e], 32)
                act.activation(w1_part[:, e, 0], w1_whole(e), ACT.Copy)
                act.activation(w2_part(e)[:, 0], w2_whole(e), ACT.Copy).then_inc(w_high, 1)

            def copy_values(g):
                act.wait_ge(pv_done, g + 1)
                if g >= 2:
                    act.wait_ge(turn_full, fold_use(g - 2))
                act.activation(oT[:, g % 2, :], av[:, :], ACT.Copy).then_inc(oT_ready, 1)

            for g in range(NG):
                t = g % 2
                if g >= 2:
                    act.wait_ge(p_low, 2 * g - 2)
                    act.wait_ge(p1_low, g - 1)
                    act.wait_ge(pv_done, g - 1)
                for pair in range(2):
                    heads = slice(2 * pair, 2 * pair + 2)
                    act.wait_ge(sc_full, 3 * g + pair + 1)
                    act.activation(p0[:, t, heads, :], sc[:, heads, :], ACT.Exp, scale=SCALE)
                    act.activation(p0_part[:, t, 0, heads, :], sc[:, heads, :], ACT.Exp,
                                   scale=SCALE).then_inc(sc_free, 1)
                if g + 1 < NG:
                    pack(g + 1)
                act.wait_ge(sc_full, 3 * g + 3)
                act.activation(p1[:, t, :], sc1[:, 0:Q1], ACT.Exp, scale=SCALE)
                act.activation(p1_part[:, t, 0, :], sc1[:, 0:Q1], ACT.Exp, scale=SCALE).then_inc(sc_free, 1)
                if g == 0:
                    split_values(2)
                if g >= 1:
                    copy_values(g - 1)
            copy_values(NG - 1)
            for e in range(SPLIT_FIRST, E):
                high_weights(e)

            for k, (t0, t1) in enumerate(blocks):
                act.wait_ge(diff_ready, k + 1)
                act.activation(ediff[:, t0:t1], diff[:, t0:t1], ACT.Exp).then_inc(ediff_ready, 1)

            def high_rows(e):
                act.wait_ge(xsT_ps, e + 1)
                if e >= 2:
                    act.wait_ge(h_ps, FC * (e - 1))
                act.activation(xsT[:, e % 2, 0, :], turn[e % 2][:, 0:SLOTS], ACT.Copy).then_inc(xsT_high, 1)

            def add_bias(e):
                act.wait_ge(yT_ps, e + 1)
                if e >= 2:
                    act.wait_ge(y_ps, e - 1)
                act.activation(yT[:, e % 2, 0:SLOTS], (sc1, av)[e % 2][:, 0:SLOTS], ACT.Identity,
                               bias=B2[:, e:e + 1]).then_inc(yT_ready, 1)

            act.activation(gelu_first[:, :], G[:, 0:1], ACT.Gelu)
            act.wait_ge(wo_in, 32)
            high_rows(0)
            for e in range(E):
                if e + 1 < E:
                    high_rows(e + 1)
                if e >= 2:
                    act.wait_ge(h_split, 2 * e - 2)
                else:
                    act.wait_ge(w_late_split, E - SPLIT_FIRST)
                for c in range(FC):
                    act.wait_ge(h_ps, FC * e + c + 1)
                    act.activation(hT[:, e % 2, c, :], sc[:, c, 0:SLOTS], ACT.Gelu,
                                   bias=B1[:, e, c:c + 1]).then_inc(h_ready, 1)
                if e:
                    add_bias(e - 1)
            add_bias(E - 1)

            n = NT // NPIECES
            act.wait_ge(weights_ready, 1)
            for c in range(NPIECES):
                act.wait_ge(yk_in[c], 16)
                for t in range(n * c, n * c + n):
                    last = act.activation(yk[:, t, 1, :], yk[:, t, 1, :], ACT.Copy, scale=weight[:, t, 1:2])
                last.then_inc(second_ready, 1)

        @block.tensor
        def _(pe):
            uses, full = [0], [0]
            occupied = [None, None]

            def bank(reader=None):
                n = uses[0] % 2
                uses[0] += 1
                if occupied[n]:
                    pe.wait_ge(*occupied[n])
                if reader is None:
                    full[0] += 1
                    reader = (turn_free, full[0])
                occupied[n] = reader
                return turn[n]

            pe.wait_ge(ctx_in, 32)
            pe.wait_ge(wk_in, 16)
            pe.matmul(sc1[:, 0:B * CP], WK[:, :], CT[:, :, 0:CP], start=True, stop=True).then_inc(kv_ps, 1)
            def queries(b):
                pe.wait_ge(xnT_ready, b + 1)
                pe.matmul(sc[:, 2 + b, :], WQ[:, :], xnT[:, b, :], start=True, stop=True).then_inc(q_ps, 1)

            def turn_rows(b):
                pe.wait_ge(xn_ready, b + 1)
                for t in range(QT):
                    mm = pe.transpose(sc[:, b, t * P:t * P + P], xn[:, QT * b + t, :], identf[:, :])
                mm.then_inc(xnT_ps, 1)

            pe.wait_ge(wq_in, 16)
            pe.wait_ge(consts1, 1)
            turn_rows(0)
            queries(0)
            pe.wait_ge(kT_split, 1)
            pe.wait_ge(pack_ready, 1)
            for i in range(4):
                if i >= 2:
                    pe.wait_ge(k_packed, i - 1)
                for part in range(2):
                    mm = pe.matmul((sc1, av)[i % 2][:, 0:B * CP],
                                   pack_k[:, part, i].rearrange("p j s d -> p (j s d)"),
                                   kT_part[:, part].rearrange("p b k -> p (b k)"), start=(part == 0),
                                   stop=(part == 1))
                mm.then_inc(k_packed_ps, 1)

            def maxima(todo):
                for b, qt, h0, nh, keys in todo:
                    ps = bank()
                    o = ps[:, 0:nh * keys].rearrange("p (h k) -> p h k", h=nh)
                    mm = pe.matmul(o, qT[:, 0, b, qt * P:qt * P + P], kTr[:, b, h0:h0 + nh, 0:keys],
                                   start=True, stop=(qt >= 2), skip_group_check=True)
                    if qt == 0:
                        mm = pe.matmul(o, identb[:, :], mask_q[:, 0:nh, :], start=False, stop=True,
                                       skip_group_check=True)
                    if qt == 1:
                        mm = pe.matmul(o[:, :, P:C], identb[:, :], mask_q[:, 0:nh, 0:C1], start=False,
                                       stop=True, skip_group_check=True)
                    mm.then_inc(turn_full, 1)

            use_of = {}

            def pack_dims(b, i, ps):
                for part in range(2):
                    pe.matmul(ps, pack_q[:, part, i].rearrange("p j s d -> p (j s d)"), qT[:, part, b, :],
                              start=(part == 0), stop=False, skip_group_check=True)

            def pack_maxima(i, ps):
                for t in range(QT):
                    mm = pe.matmul(ps[:, t * P:t * P + P],
                                   top2[:, t, 4 * i:4 * i + 4, :].rearrange("p j s -> p (j s)"), identb[:, :],
                                   start=False, stop=True, skip_group_check=True)
                return mm

            def scores(g, pair):
                b, i = divmod(g, 4)
                pe.wait_ge(q_packed, g + 1)
                if g:
                    pe.wait_ge(sc_free, 3 * g - 2 + pair)
                for j in (2 * pair, 2 * pair + 1):
                    q = slice(32 * j, 32 * j + 32)
                    pe.matmul(sc[:, j, :], k_pack[q, i, b, 0:P], q_pack[q, i, b, :], start=True, stop=False,
                              skip_group_check=True)
                    mm = pe.matmul(sc[:, j, 0:P], identb[:, :], mask_k0[:, :], start=False, stop=True,
                                   skip_group_check=True)
                mm.then_inc(sc_full, 1)

            def last_scores(g):
                b, i = divmod(g, 4)
                if g:
                    pe.wait_ge(sc_free, 3 * g)
                pe.matmul(sc1[:, 0:Q1], k1[:, b, i].rearrange("p j k -> p (j k)"), q_pack[:, i, b, P:S],
                          start=True, stop=False, skip_group_check=True)
                pe.matmul(sc1[:, 0:32], identb[:, :], mask_k1[:, :], start=False, stop=True,
                          skip_group_check=True).then_inc(sc_full, 1)

            def values(g):
                b, i = divmod(g, 4)
                if g:
                    pe.wait_ge(oT_ready, g)
                for part in range(2):
                    if part == 0:
                        pe.wait_ge(sc_free, 3 * g + 3)
                    else:
                        pe.wait_ge(p_low, 2 * g + 2)
                    for j in range(4):
                        pe.matmul(av[32 * j:32 * j + VW, :], v0[:, b, 4 * j + i, :],
                                  p0_part[:, g % 2, part, j, :], start=(part == 0), stop=False,
                                  skip_group_check=True)
                pe.wait_ge(p1_low, g + 1)
                for part in range(2):
                    mm = pe.matmul(av[:, P:S], v1[:, b, i].rearrange("p j d -> p (j d)"),
                                   p1_part[:, g % 2, part, :], start=False, stop=(part == 1),
                                   skip_group_check=True)
                mm.then_inc(pv_done, 1)

            def fold_parts(g):
                pe.wait_ge(oT_ready, g + 1)
                pe.wait_ge(fold_made, 1)
                ps = bank()
                w = 4 * OW
                for t in range(QT):
                    mm = pe.matmul(ps[:, t * w:t * w + w], oT[:, g % 2, t * P:t * P + P],
                                   fold[:, :, :].rearrange("p j d -> p (j d)"), start=(t == 0), stop=True,
                                   skip_group_check=True)
                mm.then_inc(turn_full, 1)
                use_of["fold", g] = full[0]

            def post(k, n):
                tiles = range(*blocks[k])
                here = range(len(tiles))
                if n == 0:
                    pe.wait_ge(turn_free, use_of["fold", tiles[0] // QT * 4 + 3])
                    ps = bank()
                    for c, t in zip(here, tiles):
                        mm = pe.transpose(ps[:, c * P:c * P + P],
                                          attn[:, t % QT].rearrange("p i j d -> p (i j d)"), identf[:, :])
                if n == 1:
                    pe.wait_ge(turn_free, use_of[0, k])
                    pe.wait_ge(wo_in, 32)
                    ps = bank()
                    for c, t in zip(here, tiles):
                        q = t % QT * P
                        mm = pe.matmul(ps[:, c * D:c * D + D], attnT[:, q:q + P], WO[:, :],
                                       start=(c == 0), stop=True, skip_group_check=True)
                if n == 2:
                    pe.wait_ge(rows_ready, k + 1)
                    ps = bank()
                    for c, t in zip(here, tiles):
                        mm = pe.transpose(ps[:, c * P:c * P + P], rows[:, t, 0:D], identf[:, :])
                if n == 3:
                    pe.wait_ge(turn_free, use_of[2, k])
                    pe.wait_ge(small_in, 64)
                    ps = bank()
                    for c, t in zip(here, tiles):
                        q = t % QT * P
                        mm = pe.matmul(ps[:, c * E:c * E + E], rowsT[:, q:q + P], WR[:, :],
                                       start=(c == 0), stop=True, skip_group_check=True)
                if n == 4:
                    pe.wait_ge(onehot_ready, k + 1)
                    pe.wait_ge(consts3, 2)
                    ps = bank()
                    w = TOPK * E
                    for c, t in zip(here, tiles):
                        for u in range(t + 1):
                            mm = pe.matmul(ps[:, c * w:c * w + w], ones[:, :] if u < t else upto[:, :],
                                           onehot[:, u].rearrange("p k e -> p (k e)"),
                                           start=(c == 0 and u == 0), stop=(u == t), skip_group_check=True)
                mm.then_inc(turn_full, 1)
                use_of[n, k] = full[0]

            def pack(g):
                b, i = divmod(g, 4)
                ps = bank((q_packed, g + 1))
                pack_dims(b, i, ps[:, :])
                pe.wait_ge(top_ready, g + 1)
                pack_maxima(i, ps).then_inc(q_packed_ps, 1)

            def project_values():
                pe.wait_ge(wv_in, 16)
                pe.wait_ge(ctx_rep, B)
                pe.wait_ge(k_packed, 4)
                for b in range(B):
                    pe.matmul(av[:, b * D:b * D + D], CT[:, b, 0:P], WV[:, :], start=(b == 0), stop=True,
                              skip_group_check=True)
                for b in range(B):
                    mm = pe.matmul(av[:, (B + b) * D:(B + b) * D + D], CT[:, b, P:P + 128], WV[:, :],
                                   start=False, stop=True, skip_group_check=True)
                mm.then_inc(kv_ps, 1)

            turn_rows(1)
            pe.wait_ge(consts2, 1)
            pe.wait_ge(kTr_first, 1)
            pe.wait_ge(q_high, 1)
            maxima(maxima_first[:3])
            project_values()
            maxima(maxima_first[3:])
            queries(1)
            pe.wait_ge(pack_ready, 2)
            pe.wait_ge(q_ready, 1)
            pack(0)
            pe.wait_ge(k_ready, 1)
            pe.wait_ge(consts3, 1)
            pe.wait_ge(q_ready, 2)
            for g in range(NG + 2):
                if g == 0:
                    pe.wait_ge(kTr_ready, 1)
                if g == 2:
                    pe.wait_ge(kTr_ready, 2)
                maxima(maxima_beside(g, 0))
                if g < NG:
                    scores(g, 0)
                maxima(maxima_beside(g, 1))
                if g < NG:
                    scores(g, 1)
                maxima(maxima_beside(g, 2))
                if g < NG:
                    last_scores(g)
                if g >= 2:
                    fold_parts(g - 2)
                maxima(maxima_beside(g, 3))
                for when, k, n in BESIDE:
                    if when == g:
                        post(k, n)
                if g == 1:
                    pe.wait_ge(v_ready, 5 * B)
                if 1 <= g <= NG:
                    values(g - 1)
                if g + 1 < NG:
                    pack(g + 1)
                if g == 3:
                    pe.wait_ge(k_ready, 2)
                for when, k, n in BEHIND:
                    if when == g:
                        post(k, n)
            for k, n in LATER:
                post(k, n)

            def gather(e):
                ps = turn[e % 2]
                pe.wait_ge(xs_in[e], 32)
                if e == 0:
                    pe.wait_ge(turn_free, full[0])
                if e > 1:
                    pe.wait_ge(xsT_ready, e - 1)
                for n in range(ST):
                    m = P if n < ST - 1 else LAST
                    mm = pe.transpose(ps[:, n * P:n * P + m], xs[0:m, e, n, 0:D], identf[0:m, 0:m])
                mm.then_inc(xsT_ps, 1)

            def up(e):
                if e < SPLIT_FIRST:
                    pe.wait_ge(w_split, e + 1)
                else:
                    pe.wait_ge(w_late_split, e - SPLIT_FIRST + 1)
                pe.wait_ge(xsT_ready, e + 1)
                if e == 0:
                    pe.wait_ge(sc_free, 3 * NG)
                for c in range(FC):
                    if e:
                        pe.wait_ge(h_ready, FC * (e - 1) + c + 1)
                    for wp, xp in PRODUCTS:
                        mm = pe.matmul(sc[:, c, 0:SLOTS], w1_part[:, e, wp, c * P:c * P + P],
                                       xsT[:, e % 2, xp, :], start=(wp == xp == 0), stop=(wp == 1))
                    mm.then_inc(h_ps, 1)

            def down(e):
                ps = (sc1, av)[e % 2][:, 0:SLOTS]
                if e >= 2:
                    pe.wait_ge(y_ready, e - 1)
                for c in range(FC):
                    if c % 2 == 0:
                        pe.wait_ge(h_split, 2 * e + c // 2 + 1)
                    for wp, hp in PRODUCTS:
                        mm = pe.matmul(ps, w2_part(e)[:, wp, c, :], hT_part[:, e % 2, hp, c, :],
                                       start=(c == 0 and wp == hp == 0), stop=(c == FC - 1 and wp == 1))
                mm.then_inc(yT_ps, 1)

            def turn_results(e):
                pe.wait_ge(yT_ready, e + 1)
                pe.wait_ge(padded, 1)
                for n in range(ST):
                    mm = pe.transpose((sc1, av)[e % 2][:, n * P:n * P + P], yT[:, e % 2, n * P:n * P + P],
                                      identf[:, :])
                mm.then_inc(y_ps, 1)

            gather(0)
            for e in range(E):
                if e + 1 < E:
                    gather(e + 1)
                up(e)
                if e >= 2:
                    turn_results(e - 2)
                if e:
                    down(e - 1)
            turn_results(E - 2)
            down(E - 1)
            turn_results(E - 1)

        @block.vector
        def _(dve):
            steps, uses, banks, norms = [0], [0], [0], [0]

            def step(ins):
                steps[0] += 1
                ins.then_inc(vec_step, 1)
                dve.wait_ge(vec_step, steps[0])

            def bank():
                uses[0] += 1
                dve.wait_ge(turn_full, uses[0])
                banks[0] += 1
                return turn[(banks[0] - 1) % 2]

            def pass_bank():
                banks[0] += 1

            def statistics(tiles, src):
                for t in range(*tiles):
                    last = dve.bn_stats(stats[:, t, :], src[:, t, :])
                step(last)
                for t in range(*tiles):
                    last = dve.bn_aggr(mean_var[:, t, :], stats[:, t, :])
                step(last)
                v = mean_var[:, slice(*tiles), 1]
                dve.tensor_scalar(v, v, EPS, None, ALU.add).then_inc(var_ready, 1)

            def layernorm(tiles, src, dst, ready):
                norms[0] += 1
                dve.wait_ge(rstd_ready, norms[0])
                for t in range(*tiles):
                    last = dve.tensor_scalar(dst[:, t, 0:D], src[:, t, :], mean_var[:, t, 0:1],
                                             rstd[:, t:t + 1], ALU.subtract, ALU.mult)
                last.then_inc(ready, 1)

            def maxima(todo):
                for b, qt, h0, nh, keys in todo:
                    ps = bank()
                    dve.tensor_reduce(top[:, b, qt, h0:h0 + nh],
                                      ps[:, 0:nh * keys].rearrange("p (h k) -> p h k", h=nh),
                                      AX.X, ALU.max).then_inc(turn_free, 1)

            def split_maxima(g):
                b, i = divmod(g, 4)
                dve.wait_ge(turn_free, uses[0])
                heads = slice(4 * i, 4 * i + 4)
                step(dve.tensor_copy(top2[:, :, heads, 3 * HD], top[:, b, :, heads]))
                dve.tensor_tensor(top2[:, :, heads, 3 * HD + 1], top[:, b, :, heads],
                                  top2[:, :, heads, 3 * HD], ALU.subtract).then_inc(top_ready, 1)

            def low_parts(g):
                t = g % 2
                if g >= 2:
                    dve.wait_ge(pv_done, g - 1)
                for pair in range(2):
                    dve.wait_ge(sc_free, 3 * g + pair + 1)
                    heads = slice(2 * pair, 2 * pair + 2)
                    dve.tensor_tensor(p0_part[:, t, 1, heads], p0[:, t, heads], p0_part[:, t, 0, heads],
                                      ALU.subtract).then_inc(p_low, 1)

            def normalise(g):
                ps = bank()[:, 0:QT * 4 * OW].rearrange("p (t j d) -> p t j d", t=QT, j=4)
                step(dve.reciprocal(inv[:, g], ps[:, :, :, HD]))
                dve.tensor_tensor(attn[:, :, g % 4], ps[:, :, :, 0:HD],
                                  inv[:, g].unsqueeze(3).to_broadcast([P, QT, 4, HD]),
                                  ALU.mult).then_inc(turn_free, 1)

            def copy_turned(dst, k):
                t0, t1 = blocks[k]
                ps = bank()
                dve.tensor_copy(dst[:, t0 % QT * P:t0 % QT * P + (t1 - t0) * P],
                                ps[:, 0:(t1 - t0) * P]).then_inc(turn_free, 1)

            def residual(k):
                tiles = slice(*blocks[k])
                ps = bank()
                dve.wait_ge(gate_ready, 1)
                dve.scalar_tensor_tensor(x1[:, tiles, :].rearrange("p t d -> p (t d)"),
                                         ps[:, 0:(tiles.stop - tiles.start) * D], gate[:, 0:1],
                                         X[:, tiles, :].rearrange("p t d -> p (t d)"),
                                         ALU.mult, ALU.add).then_inc(turn_free, 1)
                dve.wait_ge(turn_free, uses[0])
                statistics(blocks[k], x1)

            def choose(k):
                t0, t1 = blocks[k]
                n = t1 - t0
                cols = slice(TOPK * t0, TOPK * t1)
                ps = bank()
                dve.tensor_copy(logits[:, t0:t1, :].rearrange("p t e -> p (t e)"),
                                ps[:, 0:n * E]).then_inc(turn_free, 1)
                dve.wait_ge(turn_free, uses[0])
                for t in range(t0, t1):
                    last = dve.max(best[:, t, :], logits[:, t, :])
                step(last)
                for t in range(t0, t1):
                    last = dve.max_index(best_at[:, t, :], best[:, t, :], logits[:, t, :])
                step(last)
                step(dve.tensor_copy(chosen[:, t0:t1, :], best_at[:, t0:t1, 0:TOPK]))
                dve.wait_ge(consts3, 2)
                oh = onehot[:, t0:t1].rearrange("p t k e -> p (t k) e")
                dve.tensor_tensor(oh, expert_no[:, :].unsqueeze(1).to_broadcast([P, n * TOPK, E]),
                                  chosen[:, t0:t1, :].rearrange("p t k -> p (t k)").unsqueeze(2)
                                  .to_broadcast([P, n * TOPK, E]), ALU.is_equal).then_inc(onehot_ready, 1)
                dve.tensor_tensor(diff[:, t0:t1], best[:, t0:t1, 1], best[:, t0:t1, 0],
                                  ALU.subtract).then_inc(diff_ready, 1)
                dve.wait_ge(onehot_ready, k + 1)
                step(dve.tensor_tensor(picked[:, cols, :].rearrange("p (t k) e -> p t (k e)", k=TOPK),
                                       oh.rearrange("p (t k) e -> p t (k e)", k=TOPK),
                                       base[:, :, :].rearrange("p k e -> p (k e)").unsqueeze(1)
                                       .to_broadcast([P, n, TOPK * E]), ALU.mult))
                step(dve.tensor_reduce(first[:, cols], picked[:, cols, :], AX.X, ALU.add))

            def place(k):
                t0, t1 = blocks[k]
                cols = slice(TOPK * t0, TOPK * t1)
                ps = bank()
                dve.tensor_tensor(picked[:, cols, :],
                                  ps[:, 0:(t1 - t0) * TOPK * E].rearrange("p (c e) -> p c e", e=E),
                                  onehot[:, t0:t1].rearrange("p t k e -> p (t k) e"),
                                  ALU.mult).then_inc(turn_free, 1)
                dve.wait_ge(turn_free, uses[0])
                step(dve.tensor_reduce(rank[:, cols], picked[:, cols, :], AX.X, ALU.add))
                dve.tensor_scalar(over[:, cols], rank[:, cols], float(CAP), FAR, ALU.is_gt, ALU.mult)
                step(dve.tensor_tensor(first[:, cols], first[:, cols], rank[:, cols], ALU.add))
                dve.tensor_tensor(slot_of[:, cols], first[:, cols], over[:, cols],
                                  ALU.add).then_inc(slot_ready, 1)

            dve.memset(pack_raw[:, :, :, :, :, :, :], 0.0).then_inc(cleared, 1)
            dve.wait_ge(x_in[0], 16)
            statistics((0, QT), X)
            dve.memset(v0[:, :, :, :], 0.0)
            dve.memset(v1[:, :, :, :, :], 0.0).then_inc(cleared, 1)
            layernorm((0, QT), X, xn, xn_ready)
            dve.wait_ge(consts2, 1)
            dve.tensor_reduce(minus_one[:, :], minus_raw[:, :, :], AX.XY, ALU.add).then_inc(minus_ready, 1)
            dve.wait_ge(kT_ready, 1)
            step(dve.tensor_copy(kT_part[:, 0], kT[:, :, :]))
            dve.tensor_tensor(kT_part[:, 1], kT[:, :, :], kT_part[:, 0], ALU.subtract).then_inc(kT_split, 1)
            dve.tensor_tensor(kTr[:, 0, 0:FIRST_HEADS],
                              kT_part[:, 0, 0, 0:C].unsqueeze(1).to_broadcast([P, FIRST_HEADS, C]),
                              head_mask[:, :, :].rearrange("p i j -> p (i j)")[:, 0:FIRST_HEADS].unsqueeze(2)
                              .to_broadcast([P, FIRST_HEADS, C]), ALU.mult).then_inc(kTr_first, 1)
            dve.wait_ge(x_in[1], 16)
            statistics((QT, NT), X)
            dve.memset(top2[:, :, :, :], 0.0).then_inc(cleared, 1)
            layernorm((QT, NT), X, xn, xn_ready)

            def place_values():
                dve.wait_ge(v_part, PARTS)
                dve.wait_ge(consts3, 1)
                for b in range(B):
                    dve.tensor_copy(v0[:, b, :, 0:PARTS * HD],
                                    vs[:, b].rearrange("p h s d -> p h (s d)")).then_inc(v_ready, 1)
                for b in range(B):
                    last_keys = vs[:, B + b].rearrange("p (j i) s d -> p i j (s d)", i=4)
                    for j in range(4):
                        q = slice(32 * j, 32 * j + C1)
                        dve.tensor_copy(v1[q, b, :, j, 0:PARTS * HD], last_keys[q, :, j, :]).then_inc(v_ready, 1)

            def low_queries(b):
                dve.wait_ge(q_high, b + 1)
                dve.tensor_tensor(qT[:, 1, b, :], sc[:, 2 + b, :], qT[:, 0, b, :],
                                  ALU.subtract).then_inc(q_ready, 1)

            low_queries(0)
            dve.wait_ge(cleared, 3)
            maxima(maxima_first)
            split_maxima(0)
            pass_bank()
            low_queries(1)

            def after(k, n):
                if n == 0:
                    copy_turned(attnT, k)
                if n == 1:
                    residual(k)
                if n == 2:
                    copy_turned(rowsT, k)
                if n == 3:
                    choose(k)
                if n == 4:
                    place(k)

            for g in range(NG + 2):
                for n in range(3):
                    maxima(maxima_beside(g, n))
                    if g == n == 1:
                        place_values()
                if g >= 2:
                    normalise(g - 2)
                if g + 1 < NG:
                    maxima(maxima_beside(g, 3))
                    split_maxima(g + 1)
                for when, k, n in BESIDE:
                    if when == g:
                        after(k, n)
                if g + 1 < NG:
                    pass_bank()
                if g < NG:
                    low_parts(g)
                if (g, 0, 1) in BESIDE:
                    layernorm(blocks[0], x1, rows, rows_ready)
                for when, k, n in BEHIND:
                    if when == g:
                        after(k, n)
            for k, n in LATER:
                after(k, n)
                if (k, n) == (2, 1):
                    layernorm(blocks[1], x1, rows, rows_ready)
                    layernorm(blocks[2], x1, rows, rows_ready)

            dve.wait_ge(ediff_ready, len(blocks))
            step(dve.tensor_scalar(weight[:, :, 1], ediff[:, :], 1.0, None, ALU.add))
            step(dve.reciprocal(diff[:, :], weight[:, :, 1]))
            step(dve.tensor_scalar(weight[:, :, 0], diff[:, :], gate[:, 1:2], None, ALU.mult))
            dve.tensor_tensor(weight[:, :, 1], weight[:, :, 0], ediff[:, :], ALU.mult).then_inc(weights_ready, 1)

            def low_rows(e):
                dve.wait_ge(xsT_high, e + 1)
                dve.tensor_tensor(xsT[:, e % 2, 1, :], turn[e % 2][:, 0:SLOTS], xsT[:, e % 2, 0, :],
                                  ALU.subtract).then_inc(xsT_ready, 1)

            def results_out(e):
                dve.wait_ge(y_ps, e + 1)
                if e >= 2:
                    dve.wait_ge(back[e % 2], 16 * ST * (e // 2))
                dve.tensor_copy(y[:, e % 2, :, :], (sc1, av)[e % 2][:, 0:ST * D]
                                .rearrange("p (n d) -> p n d", d=D)).then_inc(y_ready, 1)

            def split_hidden(e):
                t = e % 2
                if e >= 2:
                    dve.wait_ge(yT_ps, e - 1)
                for c in range(0, FC, 2):
                    dve.wait_ge(h_ready, FC * e + c + 2)
                    h = hT[:, t, c:c + 2, :]
                    step(dve.tensor_copy(hT_part[:, t, 0, c:c + 2, 0:SLOTS], h))
                    dve.tensor_tensor(hT_part[:, t, 1, c:c + 2, 0:SLOTS], h, hT_part[:, t, 0, c:c + 2, 0:SLOTS],
                                      ALU.subtract).then_inc(h_split, 1)

            dve.memset(yT[:, :, SLOTS:ST * P], 0.0).then_inc(padded, 1)
            for e in range(SPLIT_FIRST, E):
                dve.wait_ge(w_high, e - SPLIT_FIRST + 1)
                dve.tensor_tensor(w1_part[:, e, 1], w1_whole(e), w1_part[:, e, 0], ALU.subtract)
                dve.tensor_tensor(w2_part(e)[:, 1], w2_whole(e), w2_part(e)[:, 0],
                                  ALU.subtract).then_inc(w_late_split, 1)
            low_rows(0)
            for e in range(E):
                if e + 1 < E:
                    low_rows(e + 1)
                if e >= 2:
                    results_out(e - 2)
                split_hidden(e)
                if e == 0:
                    for n in range(E):
                        dve.wait_ge(xs_in[n], 32)
                    dve.tensor_tensor(result_of[:, :, 0:ST - 1], xs[:, :, 0:ST - 1, D],
                                      choice_row[:, 0:ST - 1].unsqueeze(1).to_broadcast([P, E, ST - 1]),
                                      ALU.add).then_inc(result_rows, 1)
                    dve.tensor_tensor(result_of[0:LAST, :, ST - 1], xs[0:LAST, :, ST - 1, D],
                                      choice_row[0:LAST, ST - 1:ST].to_broadcast([LAST, E]),
                                      ALU.add).then_inc(result_rows, 1)
            results_out(E - 2)
            results_out(E - 1)

            n = NT // NPIECES
            for c in range(NPIECES):
                tiles = slice(n * c, n * c + n)
                dve.wait_ge(yk_in[c], 16)
                for t in range(n * c, n * c + n):
                    last = dve.scalar_tensor_tensor(fin[:, t, :], yk[:, t, 0, :], weight[:, t, 0:1],
                                                    x1[:, t, :], ALU.mult, ALU.add)
                step(last)
                dve.wait_ge(second_ready, c + 1)
                dve.tensor_tensor(fin[:, tiles, :], fin[:, tiles, :], yk[:, tiles, 1, :],
                                  ALU.add).then_inc(fin_ready, 1)


def kernel(x, ctx_1024, g_xattn, g_ffn, L0_xattn_Wq, L0_xattn_Wk, L0_xattn_Wv, L0_xattn_Wo,
           L0_ffn_Wr, L0_ffn_W1, L0_ffn_b1, L0_ffn_W2, L0_ffn_b2):
    import numpy as np
    from concourse import bacc
    from concourse.bass_utils import run_bass_kernel_spmd

    woT = np.transpose(np.reshape(L0_xattn_Wo, (D, 4, 4, HD)), (2, 1, 3, 0)).reshape(D, D)
    arrays = {
        "x": np.reshape(x, (T, D)),
        "ctxT": np.transpose(ctx_1024, (2, 0, 1)),
        "gx": g_xattn,
        "gf": g_ffn,
        "wqT": np.transpose(L0_xattn_Wq),
        "wkT": np.transpose(L0_xattn_Wk),
        "wvT": np.transpose(L0_xattn_Wv),
        "woT": woT,
        "wr": L0_ffn_Wr,
        "w1": L0_ffn_W1,
        "b1T": np.transpose(np.reshape(L0_ffn_b1, (E, FC, P)), (2, 0, 1)),
        "w2": L0_ffn_W2,
        "b2T": np.transpose(L0_ffn_b2),
    }
    nc = bacc.Bacc("TRN2", target_bir_lowering=False, num_devices=1)
    args = []
    for name, a in arrays.items():
        arrays[name] = a = np.ascontiguousarray(a)
        args.append(nc.dram_tensor(name, a.shape, mybir.dt.from_np(a.dtype), kind="ExternalInput").ap())
    out = nc.dram_tensor("out", (T, D), F32, kind="ExternalOutput").ap()
    build(nc, *args, out)
    done = run_bass_kernel_spmd(nc, [arrays], core_ids=[0])
    return done.results[0]["out"].reshape(B, S, D)
```
